# Optimizing a Trainium2 kernel written in Bass

```python
import numpy as np
import jax
import jax.numpy as jnp

def _softmax(x, axis=-1):
    return jax.nn.softmax(x, axis=axis)

def _gelu(x):
    return jax.nn.gelu(x, approximate=True)

def _silu(x):
    return jax.nn.silu(x)

def _sigmoid(x):
    return jax.nn.sigmoid(x)

def _layernorm(x, axis=-1, eps=1e-05):
    m = jnp.mean(x, axis=axis, keepdims=True)
    v = jnp.var(x, axis=axis, keepdims=True)
    return (x - m) / jnp.sqrt(v + eps)

def _scatter_add(tgt, idx, src, axis=0):
    return tgt.at[idx].add(src)

def _segment_sum(src, seg, n):
    return jax.ops.segment_sum(src, seg, n)
kernel_name = 'mk_gnn_preln_d1_gnn_r32_e59da9'

def setup_inputs(seed: int=0):
    np.random.seed(seed)
    _w = jnp.asarray

    def _rec_inputs():
        import jax
        import jax.numpy as jnp
        _gk = jax.random.key(seed)
        x = -0.0003713 + 1 * jax.random.normal(jax.random.fold_in(_gk, 1), (50000, 128), jnp.float32)
        src = jax.random.randint(jax.random.fold_in(_gk, 2), (25000,), 0, 50000, jnp.int32)
        dst = jax.random.randint(jax.random.fold_in(_gk, 3), (25000,), 0, 50000, jnp.int32)
        _o = jnp.argsort(dst, stable=True)
        src = src[_o]
        dst = dst[_o]
        edge_type_64 = jax.random.randint(jax.random.fold_in(_gk, 12), (25000,), 0, 64, jnp.int32)
        return (x, src, dst, edge_type_64)
    x, src, dst, edge_type_64 = _rec_inputs()

    def _L0_gnn_setup():
        import jax, jax.numpy as jnp
        import numpy as np
        N_HOPS = 3
        N_ENTITIES = 3125
        EMB = 128
        N_EDGES = 18750
        N_REL = 64
        key = jax.random.key(seed)
        k1, k2, k3, k4, k5, k6 = jax.random.split(key, 6)
        entity_emb = jax.random.normal(k1, (N_ENTITIES, EMB), dtype=jnp.float32)
        edge_emb = jax.random.normal(k2, (N_REL, EMB), dtype=jnp.float32)
        q_w = jax.random.normal(k3, (EMB, EMB), dtype=jnp.float32) * (1.0 / np.sqrt(EMB))
        k_w = jax.random.normal(k4, (EMB, EMB), dtype=jnp.float32) * (1.0 / np.sqrt(EMB))
        edge_index = jax.random.randint(k5, (2, N_EDGES), 0, N_ENTITIES, dtype=jnp.int64)
        edge_type = jax.random.randint(k6, (N_EDGES,), 0, N_REL, dtype=jnp.int64)
        return {'entity_emb': entity_emb, 'edge_emb': edge_emb, 'q_w': q_w, 'k_w': k_w, 'edge_index': edge_index, 'edge_type': edge_type, 'mess_dropout': 0}
    _L0_gnn_all = _L0_gnn_setup()
    _L0_gnn_in = {k: v for k, v in _L0_gnn_all.items() if k in ('edge_emb', 'q_w', 'k_w')}
    del _L0_gnn_all
    return {'x': x, 'src': src, 'dst': dst, 'edge_type_64': edge_type_64, 'L0_gnn_edge_emb': _L0_gnn_in['edge_emb'], 'L0_gnn_q_w': _L0_gnn_in['q_w'], 'L0_gnn_k_w': _L0_gnn_in['k_w']}

def reference(x, src, dst, edge_type_64, L0_gnn_edge_emb, L0_gnn_q_w, L0_gnn_k_w):
    import jax
    import jax.numpy as jnp

    def _L0_gnn_ref(entity_emb, edge_emb, q_w, k_w, edge_index, edge_type, mess_dropout):
        import jax, jax.numpy as jnp
        import numpy as np
        N_HOPS = 3
        N_ENTITIES = 3125
        EMB = 128
        N_EDGES = 18750
        N_REL = 64
        head = edge_index[0]
        tail = edge_index[1]
        rel = edge_emb[edge_type]
        n = entity_emb.shape[0]
        agg = entity_emb
        out = jnp.zeros_like(entity_emb)
        for _ in range(N_HOPS):
            h = agg[head]
            t = agg[tail]
            left = h @ q_w
            right = jnp.tanh(rel * t @ k_w)
            att = jnp.sum(left * right, axis=1)
            seg_max = jax.ops.segment_max(att, head, num_segments=n)
            e = jnp.exp(att - seg_max[head])
            seg_sum = jax.ops.segment_sum(e, head, num_segments=n)
            w = e / seg_sum[head]
            msg = w[:, None] * rel * t
            summed = jax.ops.segment_sum(msg, head, num_segments=n)
            cnt = jax.ops.segment_sum(jnp.ones_like(att), head, num_segments=n)
            agg = summed / jnp.maximum(cnt, 1.0)[:, None]
            norm = jnp.linalg.norm(agg, axis=1, keepdims=True)
            agg = agg / jnp.maximum(norm, 1e-12)
            out = out + agg + entity_emb
        return out
    edge_index = jnp.stack([src, dst])
    h = jnp.maximum(_layernorm(x, axis=-1), 0.0)
    x = x + _L0_gnn_ref(h, L0_gnn_edge_emb, L0_gnn_q_w, L0_gnn_k_w, edge_index, edge_type_64, 0)
    return x

_drawn_inputs = setup_inputs


def setup_inputs(seed=0):
    import zlib

    import numpy as np

    out = dict(_drawn_inputs(seed))
    spreads = {}
    factors = {}
    for name, (base, spread) in spreads.items():
        noise = np.random.default_rng([zlib.crc32(name.encode()), seed]).standard_normal(out[name].shape)
        drawn = base * np.exp(spread * noise) if base else spread * noise
        out[name] = jnp.asarray(drawn.astype(out[name].dtype))
    for name, factor in factors.items():
        out[name] = (out[name] * factor).astype(out[name].dtype)
    return out
```

```python
from contextlib import ExitStack

import concourse.bass as bass
from concourse import mybir

F32 = mybir.dt.float32
I32 = mybir.dt.int32
U8 = mybir.dt.uint8
ALU = mybir.AluOpType
ACT = mybir.ActivationFunctionType

N, E, D, NREL = 50000, 25000, 128, 64
HOPS = 3
R = 125
NT = E // R
P = 128
NS = NT * P
Q = NT // 2
GT = 4
NG = NT // GT
NI = NG // 2
SC = 256
LOGN = 15
DR = 125
DK = N // DR
DC = 8
ND = DK // DC
BIG = 3.0e38
EPS = 1e-5
PADKEY = 65536.0
NOSEG = 200.0
NTYPES_PAD = 64.0
LN_SUM, LN_DIF, LN_Q, LN_D2, LN_V, LN_VE, LN_SD, LN_RS, LN_NB = range(9)
NPH = LOGN - 8


def gnn_kernel(nc, x, src, dst, etype, edge_emb, q_w, k_w, out):
    ctx = ExitStack()
    with ctx:
        def sb(name, shape, dt=F32):
            return ctx.enter_context(nc.sbuf_tensor(name, shape, dt))

        def sem(name):
            return ctx.enter_context(nc.semaphore(name))

        def dram(name, shape, dt=F32):
            return nc.dram_tensor(name, shape, dt, kind="Internal").ap()

        hs_d = dram("hs_d", [32768 + 128])
        vs_d = dram("vs_d", [32768])
        lid_d = dram("lid_d", [NS], U8)
        ptab_d = dram("ptab_d", [N, 1], I32)
        rel_d = dram("rel_d", [NS, D])
        base_d = dram("base_d", [NS, D])
        left_d = [dram(f"left{k}_d", [NS, D]) for k in range(2)]
        agg_d = [dram(f"agg{k}_d", [NS + P, D]) for k in range(2)]
        bt_d = dram("bt_d", [2, NT * D])
        fx_d = dram("fx_d", [2, NT * D])

        def slots(t):
            return t[0:NS, :].rearrange("(n p) f -> p n f", p=P)

        rt = sb("rt", [P, NT, D])
        segbc = sb("segbc", [P, NT, P], U8)
        tr = sb("tr", [P, 2 * GT, D])
        xr = sb("xr", [P, 2 * GT, D])
        relr = sb("relr", [P, 2 * GT, D])
        rtr = sb("rtr", [P, 2 * GT, D])
        rtT = sb("rtT", [P, 2 * GT, D])
        thr = sb("thr", [P, 2 * GT, D])
        hr = sb("hr", [P, 2 * GT, D])
        hT = sb("hT", [P, GT, D])
        minus1 = sb("minus1", [1, 1])
        ident = sb("ident", [P, P])
        kw = sb("kw", [D, D])
        qw = sb("qw", [D, D])
        emb = sb("emb", [P, D])
        iota_c = sb("iota_c", [P, P])
        ohT = sb("ohT", [P, GT, P])
        oh = sb("oh", [P, GT, P])
        onesr = sb("onesr", [1, P])
        stats = sb("stats", [P, 2 * GT, 6])
        lns = sb("lns", [P, 2, 9, 2 * GT])
        flat = rt[:, :, :].rearrange("p n f -> p (n f)")
        kbuf = [flat[:, i * SC:(i + 1) * SC] for i in range(2)]
        kT = [flat[:, (2 + i) * SC:(3 + i) * SC] for i in range(2)]
        vbuf = flat[:, 4 * SC:5 * SC]
        vT = flat[:, 5 * SC:6 * SC]
        swapm = flat[:, 6 * SC:6 * SC + 128]
        swapd = flat[:, 7 * SC:7 * SC + 128]
        raws = [flat[:, (8 + i) * SC:(9 + i) * SC].bitcast(I32) for i in range(3)]
        sgn = [flat[:, (11 + i) * SC:(12 + i) * SC] for i in range(8)]
        xd = [flat[:, (24 + 4 * i) * SC:(28 + 4 * i) * SC].rearrange("p (n f) -> p n f", f=D) for i in range(2)]
        hd = [flat[:, (32 + 4 * i) * SC:(36 + 4 * i) * SC].rearrange("p (n f) -> p n f", f=D) for i in range(2)]
        od = [flat[:, (40 + 4 * i) * SC:(44 + 4 * i) * SC].rearrange("p (n f) -> p n f", f=D) for i in range(2)]
        pbits = sb("pbits", [P, 9], I32)
        sgnp = sb("sgnp", [P, 9])
        hp = sb("hp", [Q, 2, R + 2])
        vl = sb("vl", [Q, 2, R])
        vi = sb("vi", [Q, 2, R], I32)
        ti = sb("ti", [Q, 2, R], I32)
        gf = sb("gf", [Q, 2, R])
        gb = sb("gb", [Q, 2, R])
        gfn = sb("gfn", [Q, 2, R])
        gbn = sb("gbn", [Q, 2, R])
        def lin(ring, k, w):
            return ring[0:Q, :, :].rearrange("p n f -> p (n f)")[:, k * 2 * P:k * 2 * P + 2 * w].rearrange("p (b r) -> p b r", b=2)
        seg_x, seg_xf, seg_xb, seg_f = (lin(tr, k, R) for k in range(4))
        seg_b = lin(xr, 0, R)
        lx = [lin(xr, k, P) for k in range(1, 4)] + [lin(relr, k, P) for k in range(4)]
        LH, LT, LS, LY, LL, LF, LB = range(7)
        lid8 = sb("lid8", [Q, 2, P], U8)
        gcol = sb("gcol", [Q, 2, 2])
        rows = sb("rows", [1, 8, NT])
        G_, GN, WGF, WGB, GNEG, GNNEG, WGFN, WGBN = range(8)
        thrf = thr[0:1, :, :].rearrange("p n f -> p (n f)")
        hrf = hr[0:1, :, :].rearrange("p n f -> p (n f)")
        whrow = thrf[:, 0:NT]
        rscan = [thrf[:, (1 + k) * NT:(2 + k) * NT] for k in range(2)]
        rcar = [hrf[:, k * NT:(k + 1) * NT] for k in range(2)]
        lcol = sb("lcol", [P, NT])
        hidx = sb("hidx", [P, NT], I32)
        tidx = sb("tidx", [P, NT], I32)
        lidx = sb("lidx", [P, NT], I32)
        pidx = sb("pidx", [P, NT], I32)
        slotid = sb("slotid", [P, NT], I32)
        tycol = sb("tycol", [P, NT])
        mfl = sb("mfl", [P, 2, NT])
        invc = sb("invc", [P, NT])
        att = sb("att", [P, NT])
        wcol = sb("wcol", [P, NT])
        wfl = sb("wfl", [P, NT, 2])
        wflr = sb("wflr", [P, 2 * GT, 2])
        bcg = sb("bcg", [P, 3, NT])
        scT = relr[:, :, :].rearrange("p n f -> p (n f)")[:, 0:2 * NT].rearrange("p (k n) -> p k n", k=2)
        cT = tr[:, :, :].rearrange("p n f -> p (n f)")[:, 0:2 * NT].rearrange("p (k n) -> p k n", k=2)
        attr = sb("attr", [P, 2, GT])
        nrm = sb("nrm", [P, 2, 4, GT])
        stg = sb("stg", [P, 2, GT], I32)
        stg2 = sb("stg2", [P, 2, GT], I32)
        stgs = sb("stgs", [P, 2, GT], I32)
        stg8 = sb("stg8", [P, 2 * GT], I32)
        got8 = sb("got8", [P, 2 * GT], I32)
        btr = hr[0:Q, 0:4, :].rearrange("p (b k) f -> p b k f", b=2)
        fxr = hr[0:Q, 4:8, :].rearrange("p (b k) f -> p b k f", b=2)
        bte = thr[0:2, :, :].rearrange("a (u t) f -> a u t f", u=2)

        ps = [ctx.enter_context(nc.psum_tensor(f"ps{i}", [P, GT, D], F32)) for i in range(8)]

        s_ld = sem("s_ld")
        s_const = sem("s_const")
        s_dve = sem("s_dve")
        s_srt = sem("s_srt")
        s_part = sem("s_part")
        s_sq = sem("s_sq")
        s_pu = [sem(f"s_pu{u}") for u in range(2)]
        s_xp = sem("s_xp")
        s_seg = sem("s_seg")
        s_segp = sem("s_segp")
        s_exp = sem("s_exp")
        s_expd = sem("s_expd")
        s_wr = sem("s_wr")
        s_rd = sem("s_rd")
        s_go = sem("s_go")
        s_pt = sem("s_pt")
        s_pi = sem("s_pi")
        s_xd = [sem(f"s_xd{u}") for u in range(2)]
        s_od = [sem(f"s_od{u}") for u in range(2)]
        s_dst = sem("s_dst")
        s_dsd = sem("s_dsd")
        s_drs = sem("s_drs")
        s_dh = sem("s_dh")
        s_do = sem("s_do")
        s_t = [sem(f"s_t{u}") for u in range(2)]
        s_rl = [sem(f"s_rl{u}") for u in range(2)]
        s_cp = [sem(f"s_cp{u}") for u in range(2)]
        s_bs = [sem(f"s_bs{u}") for u in range(2)]
        s_rt = sem("s_rt")
        s_att = sem("s_att")
        s_rtT = sem("s_rtT")
        s_rtTs = sem("s_rtTs")
        s_rg = sem("s_rg")
        s_th = sem("s_th")
        s_lst = sem("s_lst")
        s_lsd = sem("s_lsd")
        s_lrs = sem("s_lrs")
        s_lh = sem("s_lh")
        s_oh = sem("s_oh")
        s_ohT = sem("s_ohT")
        s_ohTs = sem("s_ohTs")
        s_rel = sem("s_rel")
        s_rele = sem("s_rele")
        s_base = sem("s_base")
        s_hT = sem("s_hT")
        s_hTs = sem("s_hTs")
        s_left = sem("s_left")
        s_wf = sem("s_wf")
        s_bp = sem("s_bp")
        s_be = sem("s_be")
        s_bst = [sem(f"s_bst{u}") for u in range(2)]
        s_w = sem("s_w")
        s_T = sem("s_T")
        s_nr = sem("s_nr")
        s_ag = sem("s_ag")
        s_agst = [sem(f"s_agst{u}") for u in range(2)]
        s_aT = sem("s_aT")
        s_aTs = sem("s_aTs")
        s_L = sem("s_L")
        s_Le = sem("s_Le")
        s_Lst = [sem(f"s_Lst{u}") for u in range(2)]
        s_fl = [sem(f"s_fl{u}") for u in range(2)]
        s_fin = sem("s_fin")
        s_sc = [sem(f"s_sc{u}") for u in range(2)]
        s_zero = sem("s_zero")
        s_hop = sem("s_hop")
        s_pace = sem("s_pace")
        s_pool = sem("s_pool")
        s_fix = sem("s_fix")

        PADROWS = (E // SC, E % SC)
        LOADS = 0
        x_v = x.rearrange("(p n) f -> p n f", p=DR)
        out_v = out.rearrange("(p n) f -> p n f", p=DR)
        block = ctx.enter_context(nc.Block())

        def vec(i, u):
            return 2 * i + u

        def reuse(eng, sem_, value):
            if not isinstance(value, int) or value > 0:
                eng.wait_ge(sem_, value)

        N_BIDIR = 2
        SETUP_SEG = 2 + N_BIDIR + 1 + 1

        @block.sync
        def _(sp):
            whole, rest = PADROWS
            sp.wait_ge(s_zero, 1)
            for t, a in zip(raws, (src, dst, etype)):
                sp.dma_start(t[0:whole, :], a[0:whole * SC].rearrange("(p c) -> p c", c=SC)).then_inc(s_ld, 16)
                sp.dma_start(t[whole:whole + 1, 0:rest], a[whole * SC:E].rearrange("(p c) -> p c", p=1)).then_inc(s_ld, 16)
            sp.dma_start(kw[:, :], k_w[:, :]).then_inc(s_ld, 16)
            sp.dma_start(qw[:, :], q_w[:, :]).then_inc(s_ld, 16)
            sp.dma_start(emb[0:NREL, :], edge_emb[:, :]).then_inc(s_ld, 16)
            for k in range(2):
                sp.dma_start(agg_d[k][NS:NS + P, :], tr[:, 0, :]).then_inc(s_wr, 16)
            sp.wait_ge(s_const, 1)
            sp.dma_start(ptab_d[:, :].rearrange("(p n) o -> p (n o)", p=DR), flat[0:DR, 50 * SC:50 * SC + DK].bitcast(I32)).then_inc(s_pt, 16)

            def dense(i, u, first):
                g = vec(i, u)
                if not first:
                    sp.wait_ge(s_do, g - 1)
                sp.dma_start(xd[u][0:DR, :, :], x_v[:, bass.ds(g * DC, DC), :]).then_inc(s_xd[u], 16)

            def dense_out(i, u):
                g = vec(i, u)
                sp.wait_ge(s_do, g + 1)
                sp.dma_start(out_v[:, bass.ds(g * DC, DC), :], od[u][0:DR, :, :]).then_inc(s_od[u], 16)
            dense(0, 0, True)
            dense(0, 1, True)
            with sp.Fori(1, ND // 2) as i:
                for u in range(2):
                    dense_out(i - 1, u)
                    dense(i, u, False)
            for u in range(2):
                dense_out(ND // 2 - 1, u)

            sp.wait_ge(s_go, 1)
            sp.wait_ge(s_wr, 32)
            sp.dma_start(hs_d[0:1].rearrange("(a b) -> a b", a=1), minus1[:, :]).then_inc(s_wr, 16)
            sp.dma_start(hs_d[1:32769].rearrange("(p c) -> p c", c=SC), kbuf[0]).then_inc(s_wr, 16)
            sp.dma_start(vs_d.rearrange("(p c) -> p c", c=SC), vbuf).then_inc(s_wr, 16)
            sp.wait_ge(s_wr, 80)
            hs_v = bass.AP(tensor=hs_d.tensor, offset=0, ap=[[R, Q], [R * Q, 2], [1, R + 2]])
            sp.dma_start(hp[:, :, :], hs_v).then_inc(s_rd, 16)
            sp.dma_start(vl[:, :, :], vs_d[0:E].rearrange("(b q r) -> q b r", b=2, r=R)).then_inc(s_rd, 16)
            sp.wait_ge(s_go, 2)
            sp.dma_start(lid_d.rearrange("(b q r) -> q b r", b=2, r=P), lid8[:, :, :]).then_inc(s_wr, 16)
            sp.wait_ge(s_wr, 96)
            sp.dma_start(segbc[:, :, :].rearrange("p n f -> p (n f)"),
                         lid_d[:].rearrange("(a b) -> a b", a=1).broadcast_to([P, NS])).then_inc(s_rd, 16)

            wr, rd = 96, 48
            for h in range(HOPS):
                c0 = h * NG
                def phase_a(i, u, first):
                    g = vec(i, u)
                    if h == 0:
                        sp.wait_ge(s_rt, g + 1)
                        sp.dma_start(rt[:, bass.ds(g * GT, GT), :], rtr[:, u * GT:(u + 1) * GT, :]).then_inc(s_cp[u], 16)
                        sp.dma_start(slots(rel_d)[:, bass.ds(g * GT, GT), :], relr[:, u * GT:(u + 1) * GT, :]).then_inc(s_bs[u], 16)
                        sp.dma_start(slots(base_d)[:, bass.ds(g * GT, GT), :], xr[:, u * GT:(u + 1) * GT, :]).then_inc(s_bs[u], 16)

                def load_rl(i, u):
                    g = vec(i, u)
                    sp.dma_start(relr[:, u * GT:(u + 1) * GT, :], slots(rel_d)[:, bass.ds(g * GT, GT), :]).then_inc(s_rl[u], 16)
                    sp.dma_start(xr[:, u * GT:(u + 1) * GT, :], slots(left_d[h - 1])[:, bass.ds(g * GT, GT), :]).then_inc(s_rl[u], 16)

                if h == 0:
                    with sp.Fori(0, NI) as i:
                        for u in range(2):
                            phase_a(i, u, False)
                    for u in range(2):
                        sp.wait_ge(s_bs[u], 32 * NI)
                else:
                    load_rl(0, 0)
                    load_rl(0, 1)

                    def steady(i, u, last):
                        g = vec(i, u)
                        sp.wait_ge(s_rt, c0 + g + 1)
                        sp.dma_start(rt[:, bass.ds(g * GT, GT), :], rtr[:, u * GT:(u + 1) * GT, :]).then_inc(s_cp[u], 16)
                        if not last:
                            sp.wait_ge(s_att, c0 + g + 1)
                            load_rl(i + 1, u)
                    with sp.Fori(0, NI - 1) as i:
                        for u in range(2):
                            steady(i, u, False)
                    for u in range(2):
                        steady(NI - 1, u, True)
                with sp.Fori(0, NI) as i:
                    for u in range(2):
                        g = vec(i, u)
                        sp.wait_ge(s_be, c0 + g + 1)
                        sp.dma_start(bt_d[:, bass.ds(g * GT * D, GT * D)], bte[:, u, :, :].rearrange("a t f -> a (t f)")).then_inc(s_bst[u], 16)
                for u in range(2):
                    sp.wait_ge(s_bst[u], 16 * NI * (h + 1))
                for k in range(2):
                    sp.dma_start(btr[:, :, k, :], bt_d[k, :].rearrange("(b q f) -> q b f", b=2, f=D)).then_inc(s_rd, 16)
                rd += 32
                sp.wait_ge(s_fix, h + 1)
                for k in range(2):
                    sp.dma_start(fx_d[k, :].rearrange("(b q f) -> q b f", b=2, f=D), fxr[:, :, k, :]).then_inc(s_wr, 16)
                wr += 32
                sp.wait_ge(s_wr, wr)
                sp.dma_start(rt[R:R + 2, :, :].rearrange("a n f -> a (n f)"), fx_d[:, :]).then_inc(s_rd, 16)
                rd += 16

                if h < 2:
                    def store_b(g, u, agg, left):
                        if agg is not None:
                            sp.wait_ge(s_ag, c0 + agg + 1)
                            sp.dma_start(slots(agg_d[h])[:, bass.ds(agg * GT, GT), :], hr[:, u * GT:(u + 1) * GT, :]).then_inc(s_agst[u], 16)
                        if left is not None:
                            sp.wait_ge(s_Le, c0 + left + 1)
                            sp.dma_start(slots(left_d[h])[:, bass.ds(left * GT, GT), :], thr[:, u * GT:(u + 1) * GT, :]).then_inc(s_Lst[u], 16)
                    store_b(0, 0, 0, None)
                    store_b(1, 1, 1, None)
                    with sp.Fori(1, NI) as i:
                        for u in range(2):
                            g = vec(i, u)
                            store_b(g, u, g, None)
                            store_b(g, u, None, g - 2)
                    for u in range(2):
                        store_b(0, u, None, NG - 2 + u)
                    for u in range(2):
                        sp.wait_ge(s_agst[u], 16 * NI * (h + 1))
                        sp.wait_ge(s_Lst[u], 16 * NI * (h + 1))
                else:
                    def load_f(i, u):
                        g = vec(i, u)
                        for t, d in ((tr, base_d), (xr, agg_d[0]), (relr, agg_d[1])):
                            sp.dma_start(t[:, u * GT:(u + 1) * GT, :], slots(d)[:, bass.ds(g * GT, GT), :]).then_inc(s_fl[u], 16)
                    load_f(0, 0)
                    load_f(0, 1)
                    with sp.Fori(1, NI) as i:
                        for u in range(2):
                            sp.wait_ge(s_fin, vec(i, u) - 1)
                            load_f(i, u)
            for u in range(2):
                sp.wait_ge(s_sc[u], 16 * GT * NI)
                sp.wait_ge(s_od[u], 16 * (ND // 2))
                sp.wait_ge(s_bs[u], 32 * NI)

        @block.gpsimd
        def _(pool):
            def pool_wait(sem_, value):
                pool.wait_ge(sem_, value)
                pool.sem_inc(s_pace, 1)

            def reuse_pool(sem_, value):
                if not isinstance(value, int) or value > 0:
                    pool_wait(sem_, value)
            nc.gpsimd.iota(flat[0:DR, 50 * SC:50 * SC + DK].bitcast(I32), pattern=[[0, DK]], base=NS, channel_multiplier=0).then_inc(s_const, 1)
            nc.gpsimd.iota(slotid[:, :], pattern=[[P, NT]], base=0, channel_multiplier=1).then_inc(s_const, 1)
            nc.gpsimd.iota(iota_c[:, :], pattern=[[1, P]], base=0, channel_multiplier=0,
                           allow_small_or_imprecise_dtypes=True).then_inc(s_const, 1)
            nc.gpsimd.memset(ident[:, :], 1.0).then_inc(s_const, 1)
            pool.wait_ge(s_const, 4)
            nc.gpsimd.affine_select(ident[:, :], ident[:, :], pattern=[[1, P]], base=0, channel_multiplier=-1,
                                    compare_op=ALU.is_equal, fill=0.0).then_inc(s_const, 1)
            for k in range(1, 8):
                nc.gpsimd.iota(sgn[k], pattern=[[0, SC >> (k + 1)], [-2, 2], [0, 1 << k]], base=1, channel_multiplier=0,
                               allow_small_or_imprecise_dtypes=True).then_inc(s_const, 1)
            nc.gpsimd.iota(pbits[:, 8:9], pattern=[[0, 1]], base=0, channel_multiplier=1).then_inc(s_const, 1)

            pool_wait(s_go, 3)
            pool_wait(s_pt, 16)

            def stage(dst_, src_):
                return nc.gpsimd.tensor_copy(dst_, src_)

            def table(i):
                for u in range(2):
                    g = vec(i, u)
                    reuse_pool(s_pu[u], 16 * GT * i)
                    stage(stg[:, u, :], lidx[:, bass.ds(g * GT, GT)]).then_inc(s_pool, 1)
                    stage(stgs[:, u, :], slotid[:, bass.ds(g * GT, GT)]).then_inc(s_pool, 1)
                    pool_wait(s_pool, 2 * g + 2)
                    for t in range(GT):
                        nc.gpsimd.indirect_dma_start(out=ptab_d[:, :], out_offset=bass.IndirectOffsetOnAxis(ap=stg[:, u, t:t + 1], axis=0),
                                                     in_=stgs[:, u, t:t + 1], in_offset=None, bounds_check=N - 1,
                                                     oob_is_err=False).then_inc(s_pu[u], 16)
            table(0)
            with pool.Fori(1, NI) as i:
                table(i)
            for u in range(2):
                pool_wait(s_pu[u], 16 * GT * NI)
            pb = 2 * NG
            pool_wait(s_go, 4)

            def gather1(i, u, first):
                g = vec(i, u)
                if not first:
                    pool_wait(s_att, g - 1)
                    pool_wait(s_bs[u], 32 * i)
                stage(stg[:, u, :], tidx[:, bass.ds(g * GT, GT)]).then_inc(s_pool, 1)
                stage(stg2[:, u, :], hidx[:, bass.ds(g * GT, GT)]).then_inc(s_pool, 1)
                pool_wait(s_pool, pb + 2 * g + 2)
                for t in range(GT):
                    nc.gpsimd.indirect_dma_start(out=tr[:, u * GT + t, :], out_offset=None, in_=x[:, :],
                                                 in_offset=bass.IndirectOffsetOnAxis(ap=stg[:, u, t:t + 1], axis=0)).then_inc(s_t[u], 16)
                    nc.gpsimd.indirect_dma_start(out=xr[:, u * GT + t, :], out_offset=None, in_=x[:, :],
                                                 in_offset=bass.IndirectOffsetOnAxis(ap=stg2[:, u, t:t + 1], axis=0)).then_inc(s_t[u], 16)
            gather1(0, 0, True)
            gather1(0, 1, True)
            with pool.Fori(1, NI) as i:
                for u in range(2):
                    gather1(i, u, False)
            pb += 2 * NG

            with pool.Fori(0, NT // 8) as i:
                stage(stg8[:, :], tidx[:, bass.ds(i * 8, 8)]).then_inc(s_pool, 1)
                pool_wait(s_pool, pb + 2 * i + 1)
                for t in range(8):
                    nc.gpsimd.indirect_dma_start(out=got8[:, t:t + 1], out_offset=None, in_=ptab_d[:, :],
                                                 in_offset=bass.IndirectOffsetOnAxis(ap=stg8[:, t:t + 1], axis=0)).then_inc(s_pi, 16)
                pool_wait(s_pi, 128 * i + 128)
                stage(pidx[:, bass.ds(i * 8, 8)], got8[:, :]).then_inc(s_pool, 1)
            pb += 2 * (NT // 8)
            pool_wait(s_pool, pb)

            for h in range(1, HOPS):
                for u in range(2):
                    pool_wait(s_agst[u], 16 * NI * h)
                pool_wait(s_Le, NG * h)
                tb = 2 * GT * 16 * NI + (h - 1) * GT * 16 * NI
                with pool.Fori(0, NI) as i:
                    for u in range(2):
                        g = vec(i, u)
                        pool_wait(s_rt, h * NG + g - 1)
                        stage(stg[:, u, :], pidx[:, bass.ds(g * GT, GT)]).then_inc(s_pool, 1)
                        pool_wait(s_pool, pb + g + 1)
                        for t in range(GT):
                            nc.gpsimd.indirect_dma_start(out=tr[:, u * GT + t, :], out_offset=None, in_=agg_d[h - 1][:, :],
                                                         in_offset=bass.IndirectOffsetOnAxis(ap=stg[:, u, t:t + 1], axis=0)).then_inc(s_t[u], 16)
                pb += NG

            pool_wait(s_rt, HOPS * NG)
            for u in range(2):
                pool_wait(s_od[u], 16 * (ND // 2))

            def scatter(i, u, first):
                g = vec(i, u)
                if not first:
                    pool_wait(s_sc[u], 16 * GT * i)
                stage(stg[:, u, :], lidx[:, bass.ds(g * GT, GT)]).then_inc(s_pool, 1)
                pool_wait(s_pool, pb + g + 1)
                pool_wait(s_fin, g + 1)
                for t in range(GT):
                    nc.gpsimd.indirect_dma_start(out=out[:, :], out_offset=bass.IndirectOffsetOnAxis(ap=stg[:, u, t:t + 1], axis=0),
                                                 in_=rtr[:, u * GT + t, :], in_offset=None, bounds_check=N - 1,
                                                 oob_is_err=False).then_inc(s_sc[u], 16)
            scatter(0, 0, True)
            scatter(0, 1, True)
            with pool.Fori(1, NI) as i:
                for u in range(2):
                    scatter(i, u, False)

        @block.vector
        def _(dve):
            V = nc.vector

            class Chain:
                at = 0

                def note(self, ins):
                    self.at = self.at + 1
                    ins.then_inc(s_dve, 1)

                def join(self):
                    dve.wait_ge(s_dve, self.at)

                def __call__(self, ins):
                    self.note(ins)
                    self.join()
            ch = Chain()

            ch.note(V.memset(minus1[:, :], -1.0))
            ch.note(V.memset(onesr[:, :], 1.0))
            ch.note(V.memset(raws[0], int(PADKEY)))
            ch.note(V.memset(raws[1], 0))
            ch.note(V.memset(raws[2], 0))
            ch.note(V.memset(emb[:, :], 0.0))
            ch(V.memset(tr[:, 0, :], 0.0))
            dve.sem_inc(s_zero, 1)

            def ln_small(pr, u, n, s_ask, s_got, got_at, s_out):
                def L(k):
                    return lns[0:pr, u, k, 0:n]
                me, qe, mo, qo = (stats[0:pr, 0:n, k] for k in (1, 2, 4, 5))
                ch.note(V.tensor_tensor(L(LN_SUM), me, mo, ALU.add))
                ch.note(V.tensor_tensor(L(LN_DIF), me, mo, ALU.subtract))
                ch(V.tensor_tensor(L(LN_Q), qe, qo, ALU.add))
                ch(V.tensor_tensor(L(LN_D2), L(LN_DIF), L(LN_DIF), ALU.mult))
                ch(V.scalar_tensor_tensor(L(LN_V), L(LN_D2), D / 4.0, L(LN_Q), ALU.mult, ALU.add))
                V.tensor_scalar(L(LN_VE), L(LN_V), 1.0 / D, EPS, ALU.mult, ALU.add).then_inc(s_ask, 1)
                dve.wait_ge(s_got, got_at)
                ch(V.reciprocal(L(LN_RS), L(LN_SD)))
                V.scalar_tensor_tensor(L(LN_NB), L(LN_SUM), -0.5, L(LN_RS), ALU.mult, ALU.mult).then_inc(s_out, 1)

            def dense_in(i, u):
                g = vec(i, u)
                dve.wait_ge(s_xd[u], 16 * i + 16)
                for t in range(DC):
                    ch.note(V.bn_stats(stats[0:DR, t, :], xd[u][0:DR, t, :]))
                ch.join()
                ln_small(DR, u, DC, s_dst, s_dsd, g + 1, s_drs)

            def dense_sum(i, u):
                g = vec(i, u)
                dve.wait_ge(s_dh, g + 1)
                reuse(dve, s_od[u], 16 * i)
                V.scalar_tensor_tensor(od[u][0:DR].rearrange("p n f -> p (n f)"), hd[u][0:DR].rearrange("p n f -> p (n f)"), 3.0,
                                       xd[u][0:DR].rearrange("p n f -> p (n f)"), ALU.mult, ALU.add).then_inc(s_do, 1)
            start = ch.at
            dense_in(0, 0)
            dense_in(0, 1)
            dense_sum(0, 0)
            per = ch.at - start

            def dense_step(i):
                ch.at = start + i * per
                dense_in(i, 0)
                dense_sum(i - 1, 1)
                dense_in(i, 1)
                dense_sum(i, 0)
            dense_step(1)
            with dve.Fori(2, ND // 2) as i:
                dense_step(i)
            dense_sum(ND // 2 - 1, 1)
            ch.at = start + per * (ND // 2)

            dve.wait_ge(s_ld, 16 * 9)
            ch.note(V.tensor_copy(kbuf[0], raws[0]))
            ch.note(V.scalar_tensor_tensor(vbuf, raws[1], float(NREL), raws[2], ALU.mult, ALU.add))
            dve.wait_ge(s_const, 13)
            for k in range(8):
                ch.note(V.tensor_scalar(pbits[:, k:k + 1], pbits[:, 8:9], k, 1, ALU.logical_shift_right, ALU.bitwise_and))
            ch.join()
            ch(V.tensor_scalar(sgnp[:, 0:8], pbits[:, 0:8], -2.0, 1.0, ALU.mult, ALU.add))

            def exchange(a_buf, b_buf, v, stride):
                def halves(t):
                    w = t.rearrange("p (n t s) -> p n t s", t=2, s=stride)
                    return w[:, :, 0, :], w[:, :, 1, :]
                ka, kb = halves(a_buf)
                na, nb = halves(b_buf)
                va, vb = halves(v)
                m = swapm.rearrange("p (n s) -> p n s", s=stride)
                d = swapd.rearrange("p (n s) -> p n s", s=stride)
                ch.note(V.tensor_tensor(m, ka, kb, ALU.is_gt))
                ch.note(V.tensor_tensor(d, vb, va, ALU.subtract))
                ch.note(V.tensor_tensor(na, ka, kb, ALU.min))
                dve.wait_ge(s_dve, ch.at - 1)
                ch.note(V.tensor_tensor(d, d, m, ALU.mult))
                ch.note(V.tensor_tensor(nb, ka, kb, ALU.max))
                dve.wait_ge(s_dve, ch.at - 1)
                ch.note(V.tensor_tensor(va, va, d, ALU.add))
                ch(V.tensor_tensor(vb, vb, d, ALU.subtract))

            def apply_sign(t, k):
                if 1 <= k < 8:
                    ch(V.tensor_tensor(t, t, sgn[k], ALU.mult))
                elif 8 <= k < LOGN:
                    ch(V.tensor_scalar(t, t, sgnp[:, k - 8:k - 7], None, ALU.mult))

            at, hand = 0, 0
            for k in range(1, LOGN + 1):
                apply_sign(kbuf[at], k - 1)
                apply_sign(kbuf[at], k)
                if k > 8:
                    dve.sem_inc(s_srt, 1)
                    hand += 1
                    dve.wait_ge(s_xp, hand)
                    bt = (k - 8) % 2
                    ch.note(V.tensor_copy(kT[bt], ps[0][:, 0:2, :].rearrange("p n f -> p (n f)")))
                    ch(V.tensor_copy(vT, ps[1][:, 0:2, :].rearrange("p n f -> p (n f)")))
                    for m in range(k - 1, 7, -1):
                        exchange(kT[bt], kT[1 - bt], vT, 1 << (m - 8))
                        bt = 1 - bt
                    dve.sem_inc(s_srt, 1)
                    hand += 1
                    dve.wait_ge(s_xp, hand)
                    ch.note(V.tensor_copy(kbuf[0], ps[0][:, 0:2, :].rearrange("p n f -> p (n f)")))
                    ch(V.tensor_copy(vbuf, ps[1][:, 0:2, :].rearrange("p n f -> p (n f)")))
                for m in range(min(k, 8) - 1, -1, -1):
                    exchange(kbuf[at], kbuf[1 - at], vbuf, 1 << m)
                    at = 1 - at
            assert at == 0
            dve.sem_inc(s_go, 1)

            dve.wait_ge(s_rd, 32)
            cur, first, last_ = hp[:, :, 1:R + 1], hp[:, :, 1:2], hp[:, :, R:R + 1]
            ch.note(V.tensor_tensor(gf[:, :, :], hp[:, :, 0:R], cur, ALU.is_equal))
            ch.note(V.tensor_tensor(gb[:, :, :], hp[:, :, 2:R + 2], cur, ALU.is_equal))
            ch(V.tensor_copy(vi[:, :, :], vl[:, :, :]))
            ch.note(V.tensor_copy(gcol[:, 0, :], gf[:, :, 0:1].rearrange("p b o -> p (b o)")))
            V.tensor_tensor(gcol[:, 1, :], first.rearrange("p b o -> p (b o)"), last_.rearrange("p b o -> p (b o)"),
                            ALU.is_equal).then_inc(s_seg, 1)
            ch.note(V.scalar_tensor_tensor(lx[LL][:, :, 0:R], gb[:, :, :], PADKEY, cur, ALU.mult, ALU.add))
            ch.note(V.memset(lx[LL][:, :, R:P], PADKEY))
            ch.note(V.tensor_copy(lx[LH][:, :, 0:R], cur))
            ch.note(V.memset(lx[LH][:, :, R:P], 0.0))
            ch.note(V.memset(lx[LT][:, :, R:P], 0.0))
            ch.note(V.memset(lx[LY][:, :, R:P], NTYPES_PAD))
            ch.note(V.tensor_tensor(lx[LF][:, :, 0:R], cur, first.to_broadcast([Q, 2, R]), ALU.is_equal))
            ch.note(V.tensor_tensor(lx[LB][:, :, 0:R], cur, last_.to_broadcast([Q, 2, R]), ALU.is_equal))
            ch.note(V.memset(lx[LF][:, :, R:P], 0.0))
            ch.note(V.memset(lx[LB][:, :, R:P], 0.0))
            ch.note(V.tensor_scalar(ti[:, :, :], vi[:, :, :], 6, None, ALU.logical_shift_right))
            ch(V.tensor_scalar(vi[:, :, :], vi[:, :, :], NREL - 1, None, ALU.bitwise_and))
            ch.note(V.tensor_copy(lx[LT][:, :, 0:R], ti[:, :, :]))
            ch.note(V.tensor_copy(lx[LY][:, :, 0:R], vi[:, :, :]))
            ch.note(V.tensor_scalar(seg_x, gf[:, :, :], -1.0, 1.0, ALU.mult, ALU.add))
            ch(V.memset(seg_xf, 1.0))
            ch.note(V.memset(seg_x[:, :, 0:1], 0.0))
            ch.note(V.memset(seg_xf[:, :, 0:1], 0.0))
            ch.note(V.memset(gf[:, :, 0:1], 0.0))
            ch(V.memset(gb[:, :, R - 1:R], 0.0))
            flat2 = "p b r -> p (b r)"
            ch(V.tensor_tensor_scan(seg_f.rearrange(flat2), seg_xf.rearrange(flat2), seg_x.rearrange(flat2), 0.0, ALU.mult, ALU.add))
            ch.note(V.tensor_copy(lx[LS][:, :, 0:R], seg_f))
            ch.note(V.memset(lx[LS][:, :, R:R + 1], 0.0))
            ch.note(V.tensor_copy(lx[LS][:, :, R + 1:R + 2], seg_f[:, :, R - 1:R]))
            ch.note(V.memset(lx[LS][:, :, R + 2:P], NOSEG))
            ch.note(V.tensor_scalar(gfn[:, :, :], gf[:, :, :], BIG, -BIG, ALU.mult, ALU.add))
            ch(V.tensor_scalar(gbn[:, :, :], gb[:, :, :], BIG, -BIG, ALU.mult, ALU.add))
            V.tensor_copy(lid8[:, :, :], lx[LS]).then_inc(s_go, 1)
            dve.wait_ge(s_segp, 1)
            row = ps[4][0:1, :, :].rearrange("p n f -> p (n f)")
            ch.note(V.tensor_copy(rows[:, G_, :], row[:, 0:NT]))
            ch(V.tensor_copy(whrow, row[:, NT:2 * NT]))
            ch.note(V.tensor_copy(rows[:, GN, 0:NT - 1], rows[:, G_, 1:NT]))
            ch(V.memset(rows[:, GN, NT - 1:NT], 0.0))
            ch.note(V.tensor_tensor(rows[:, WGF, :], rows[:, G_, :], whrow, ALU.mult))
            ch(V.tensor_tensor(rows[:, WGB, :], rows[:, GN, :], whrow, ALU.mult))
            for a, b in ((G_, GNEG), (GN, GNNEG), (WGF, WGFN), (WGB, WGBN)):
                ch.note(V.tensor_scalar(rows[:, b, :], rows[:, a, :], BIG, -BIG, ALU.mult, ALU.add))
            ch.join()
            dve.sem_inc(s_seg, 1)
            dve.wait_ge(s_segp, 2)

            def tile_of(k):
                return ps[k // 2][:, :, :].rearrange("p n f -> p (n f)")[:, (k % 2) * NT:(k % 2 + 1) * NT]
            ch.note(V.tensor_copy(hidx[:, :], tile_of(LH)))
            ch.note(V.tensor_copy(tidx[:, :], tile_of(LT)))
            ch.note(V.tensor_copy(lcol[:, :], tile_of(LS)))
            ch.note(V.tensor_copy(tycol[:, :], tile_of(LY)))
            ch.note(V.tensor_copy(lidx[:, :], tile_of(LL)))
            ch.note(V.tensor_copy(mfl[:, 0, :], tile_of(LF)))
            ch.note(V.tensor_copy(mfl[:, 1, :], tile_of(LB)))
            ch.note(V.tensor_copy(bcg[:, 0:2, :], ps[5][:, :, :].rearrange("p n f -> p (n f)")[:, 0:2 * NT].rearrange("p (k n) -> p k n", k=2)))
            ch(V.tensor_copy(bcg[:, 2, :], ps[6][:, :, :].rearrange("p n f -> p (n f)")[:, 0:NT]))
            dve.sem_inc(s_go, 1)

            segs = [2]

            def to_pe():
                dve.sem_inc(s_seg, 1)
                segs[0] += 1
                dve.wait_ge(s_segp, segs[0])

            def whole_segments(add, xin):
                op0, op1 = (ALU.mult, ALU.add) if add else (ALU.add, ALU.max)
                GFt, GBt = (gf, gb) if add else (gfn, gbn)
                rg, rgn, rwf, rwb = (G_, GN, WGF, WGB) if add else (GNEG, GNNEG, WGFN, WGBN)
                none = 0.0 if add else -BIG
                fl, bl = (lambda t: t.rearrange(flat2)), (lambda t: t.rearrange(flat2)[:, ::-1])
                ch.note(V.tensor_copy(seg_xf, xin))
                ch.note(V.tensor_copy(seg_xb, xin))
                ch.note(V.tensor_tensor_scan(fl(seg_f), fl(GFt[:, :, :]), fl(xin), none, op0, op1))
                ch(V.tensor_tensor_scan(bl(seg_b), bl(GBt[:, :, :]), bl(xin), none, op0, op1))
                to_pe()
                ch.note(V.tensor_tensor_scan(rscan[0], rows[:, rwf, :], row[:, 0:NT], none, op0, op1))
                ch.note(V.tensor_tensor_scan(rscan[1][:, ::-1], rows[:, rwb, ::-1], row[:, NT:2 * NT][:, ::-1], none, op0, op1))
                ch.note(V.memset(rcar[0][:, 0:1], none))
                ch.note(V.memset(rcar[1][:, NT - 1:NT], none))
                ch.join()
                ch.note(V.tensor_tensor(rcar[0][:, 1:NT], rows[:, rg, 1:NT], rscan[0][:, 0:NT - 1], op0))
                ch(V.tensor_tensor(rcar[1][:, 0:NT - 1], rows[:, rgn, 0:NT - 1], rscan[1][:, 1:NT], op0))
                to_pe()
                car = ps[4][0:Q, :, :].rearrange("p n f -> p (n f)")
                ch.note(V.tensor_tensor(seg_xf[:, :, 0], xin[:, :, 0], car[:, 400:402], op1))
                ch(V.tensor_tensor(seg_xb[:, :, R - 1], xin[:, :, R - 1], car[:, 402:404], op1))
                ch.note(V.tensor_tensor_scan(fl(seg_f), fl(GFt[:, :, :]), fl(seg_xf), none, op0, op1))
                ch(V.tensor_tensor_scan(bl(seg_b), bl(GBt[:, :, :]), bl(seg_xb), none, op0, op1))
                ch(V.tensor_tensor(seg_f, seg_f, seg_b, op1))
                if add:
                    ch(V.tensor_tensor(seg_f, seg_f, xin, ALU.subtract))

            ch(V.memset(seg_x, 1.0))
            whole_segments(True, seg_x)
            ch(V.tensor_scalar(seg_f, seg_f, 1.0, None, ALU.max))
            ch.note(V.reciprocal(lx[0][:, :, 0:R], seg_f))
            ch(V.memset(lx[0][:, :, R:P], 1.0))
            to_pe()
            ch(V.tensor_copy(invc[:, :], ps[0][:, :, :].rearrange("p n f -> p (n f)")[:, 0:NT]))
            dve.sem_inc(s_go, 1)

            for h in range(HOPS):
                c0 = h * NG
                tb = 2 * GT * 16 * NI + (h - 1) * GT * 16 * NI

                def edges(i, u):
                    g = vec(i, u)
                    s = slice(u * GT, (u + 1) * GT)
                    f = "p n f -> p (n f)"
                    if h == 0:
                        dve.wait_ge(s_t[u], 2 * GT * 16 * (i + 1))
                        for t in range(GT):
                            ch.note(V.bn_stats(stats[:, t, :], tr[:, u * GT + t, :]))
                            ch.note(V.bn_stats(stats[:, GT + t, :], xr[:, u * GT + t, :]))
                        ch.join()
                        ln_small(P, u, 2 * GT, s_lst, s_lsd, g + 1, s_lrs)
                        for t in range(GT):
                            ins = V.tensor_scalar(oh[:, t, :], iota_c[:, :], tycol[:, bass.ds(g * GT + t, 1)], None, ALU.is_equal)
                        ins.then_inc(s_oh, 1)
                        dve.wait_ge(s_lh, g + 1)
                        ch.note(V.scalar_tensor_tensor(xr[:, s, :].rearrange(f), hr[:, s, :].rearrange(f), 3.0,
                                                       xr[:, s, :].rearrange(f), ALU.mult, ALU.add))
                        dve.wait_ge(s_rel, g + 1)
                        reuse(dve, s_bs[u], 32 * i)
                        ins = V.tensor_copy(relr[:, s, :], ps[7][:, :, :])
                        ins.then_inc(s_rele, 1)
                        dve.wait_ge(s_rele, g + 1)
                        reuse(dve, s_cp[u], 16 * i)
                    else:
                        dve.wait_ge(s_t[u], tb + GT * 16 * (i + 1))
                        dve.wait_ge(s_rl[u], 32 * ((h - 1) * NI + i + 1))
                        dve.wait_ge(s_cp[u], 16 * (h * NI + i))
                    V.tensor_tensor(rtr[:, s, :], tr[:, s, :], relr[:, s, :], ALU.mult).then_inc(s_rt, 1)

                def score(i, u):
                    g = vec(i, u)
                    dve.wait_ge(s_th, c0 + g + 1)
                    if h == 0:
                        dve.wait_ge(s_left, g + 1)
                    for t in range(GT):
                        k = u * GT + t
                        left = ps[5][:, t, :] if h == 0 else xr[:, k, :]
                        ch.note(V.scalar_tensor_tensor(thr[:, k, :], thr[:, k, :], 1.0, left, ALU.mult, ALU.mult,
                                                       accum_out=attr[:, u, t:t + 1]))
                    ch.join()
                    V.tensor_copy(att[:, bass.ds(g * GT, GT)], attr[:, u, :]).then_inc(s_att, 1)
                start = ch.at
                edges(0, 0)
                edges(0, 1)
                score(0, 0)
                mid = ch.at
                score_links = GT
                per = mid - start + score_links
                with dve.Fori(1, NI) as i:
                    ch.at = start + i * per - score_links
                    edges(i, 0)
                    score(i - 1, 1)
                    edges(i, 1)
                    score(i, 0)
                ch.at = start + NI * per - score_links
                score(NI - 1, 1)

                dve.wait_ge(s_att, c0 + NG)
                if h == 0:
                    for u in range(2):
                        dve.wait_ge(s_bs[u], 32 * NI)
                to_pe()
                lin4 = ps[4][0:Q, 0:2, 0:R]
                ch(V.tensor_copy(seg_x, lin4))
                whole_segments(False, seg_x)
                V.tensor_tensor(seg_x, seg_x, seg_f, ALU.subtract).then_inc(s_exp, 1)
                dve.wait_ge(s_expd, h + 1)
                whole_segments(True, seg_x)
                ch(V.reciprocal(seg_f, seg_f))
                ch.note(V.tensor_tensor(lx[0][:, :, 0:R], seg_x, seg_f, ALU.mult))
                ch.note(V.memset(lx[0][:, :, R:R + 2], 1.0))
                ch(V.memset(lx[0][:, :, R + 2:P], 0.0))
                to_pe()
                ch(V.tensor_copy(wcol[:, :], ps[0][:, :, :].rearrange("p n f -> p (n f)")[:, 0:NT]))
                ch.note(V.tensor_tensor(wfl[:, :, 0], wcol[:, :], mfl[:, 0, :], ALU.mult))
                ch(V.tensor_tensor(wfl[:, :, 1], wcol[:, :], mfl[:, 1, :], ALU.mult))

                def partial(i, u, first=False):
                    g = vec(i, u)
                    if not first:
                        dve.wait_ge(s_bp, c0 + g - 1)
                    V.tensor_copy(wflr[:, u * GT:(u + 1) * GT, :], wfl[:, bass.ds(g * GT, GT), :]).then_inc(s_wf, 1)
                partial(0, 0, True)
                partial(0, 1, True)
                with dve.Fori(1, NI) as i:
                    partial(i, 0)
                    partial(i, 1)

                dve.wait_ge(s_part, h + 1)
                part = ps[4][:, :, :].rearrange("p n f -> p (n f)")
                ch.note(V.tensor_tensor_scan(scT[:, 0, :], bcg[:, 0, :], part[:, NT:2 * NT], 0.0, ALU.mult, ALU.add))
                ch.note(V.tensor_tensor_scan(scT[:, 1, ::-1], bcg[:, 1, ::-1], part[:, 0:NT][:, ::-1], 0.0, ALU.mult, ALU.add))
                ch.note(V.memset(cT[:, 0, 0:1], 0.0))
                ch(V.memset(cT[:, 1, NT - 1:NT], 0.0))
                ch.note(V.tensor_tensor(cT[:, 0, 1:NT], bcg[:, 2, 1:NT], scT[:, 0, 0:NT - 1], ALU.mult))
                ch(V.tensor_tensor(cT[:, 1, 0:NT - 1], bcg[:, 2, 1:NT], scT[:, 1, 1:NT], ALU.mult))
                to_pe()
                V.tensor_copy(fxr.rearrange("p b k f -> p (b k) f"), ps[5][0:Q, :, :]).then_inc(s_fix, 1)

                def weights(i, u, first=False):
                    g = vec(i, u)
                    if not first:
                        dve.wait_ge(s_T, c0 + g - 1)
                    for t in range(GT):
                        ins = V.tensor_scalar(rtT[:, u * GT + t, :], segbc[:, bass.ds(g * GT + t, 1), :].rearrange("p a f -> p (a f)"),
                                              lcol[:, bass.ds(g * GT + t, 1)], wcol[:, bass.ds(g * GT + t, 1)], ALU.is_equal, ALU.mult)
                    ins.then_inc(s_w, 1)

                def aggregate(i, u):
                    g = vec(i, u)
                    s = slice(u * GT, (u + 1) * GT)
                    dve.wait_ge(s_nr, c0 + g + 1)
                    ch(V.tensor_scalar(nrm[:, u, 1, :], nrm[:, u, 1, :], 1e-12, None, ALU.max))
                    ch(V.reciprocal(nrm[:, u, 2, :], nrm[:, u, 1, :]))
                    ch(V.tensor_tensor(nrm[:, u, 3, :], nrm[:, u, 2, :], invc[:, bass.ds(g * GT, GT)], ALU.mult))
                    if h < HOPS - 1:
                        reuse(dve, s_agst[u], 16 * (h * NI + i))
                    V.tensor_tensor(hr[:, s, :], ps[u][:, :, :], nrm[:, u, 3, :].unsqueeze(2).to_broadcast([P, GT, D]), ALU.mult).then_inc(s_ag, 1)
                    if h == HOPS - 1:
                        f = "p n f -> p (n f)"
                        dve.wait_ge(s_fl[u], 48 * (i + 1))
                        reuse(dve, s_sc[u], GT * 16 * i)
                        ch.note(V.tensor_tensor(rtr[:, s, :], tr[:, s, :], xr[:, s, :], ALU.add))
                        dve.wait_ge(s_ag, c0 + g + 1)
                        ch(V.tensor_tensor(hr[:, s, :], hr[:, s, :], relr[:, s, :], ALU.add))
                        V.tensor_tensor(rtr[:, s, :], rtr[:, s, :], hr[:, s, :], ALU.add).then_inc(s_fin, 1)

                def left_out(i, u):
                    g = vec(i, u)
                    dve.wait_ge(s_L, c0 + g + 1)
                    reuse(dve, s_Lst[u], 16 * (h * NI + i))
                    V.tensor_copy(thr[:, u * GT:(u + 1) * GT, :], ps[4 + u][:, :, :]).then_inc(s_Le, 1)
                start = ch.at
                weights(0, 0, True)
                weights(0, 1, True)
                aggregate(0, 0)
                ag_links = ch.at - start
                per = 2 * ag_links

                def sum_step(i):
                    ch.at = start + i * per - ag_links
                    weights(i, 0)
                    aggregate(i - 1, 1)
                    if h < HOPS - 1:
                        left_out(i - 1, 0)
                    weights(i, 1)
                    aggregate(i, 0)
                    if h < HOPS - 1:
                        left_out(i - 1, 1)
                sum_step(1)
                with dve.Fori(2, NI) as i:
                    sum_step(i)
                ch.at = start + NI * per - ag_links
                aggregate(NI - 1, 1)
                if h < HOPS - 1:
                    left_out(NI - 1, 0)
                    left_out(NI - 1, 1)

        @block.scalar
        def _(act):
            A = nc.scalar

            def relu_rows(pr, u, src_, dst_, n0, n):
                for t in range(n):
                    ins = A.activation(dst_[0:pr, t, :], src_[0:pr, t, :], ACT.Relu, bias=lns[0:pr, u, LN_NB, n0 + t:n0 + t + 1],
                                       scale=lns[0:pr, u, LN_RS, n0 + t:n0 + t + 1])
                return ins

            with act.Fori(0, ND // 2) as i:
                for u in range(2):
                    g = vec(i, u)
                    act.wait_ge(s_dst, g + 1)
                    A.activation(lns[0:DR, u, LN_SD, 0:DC], lns[0:DR, u, LN_VE, 0:DC], ACT.Sqrt).then_inc(s_dsd, 1)
                    act.wait_ge(s_drs, g + 1)
                    relu_rows(DR, u, xd[u], hd[u], 0, DC).then_inc(s_dh, 1)

            for h in range(HOPS):
                c0 = h * NG
                with act.Fori(0, NI) as i:
                    for u in range(2):
                        g = vec(i, u)
                        s = slice(u * GT, (u + 1) * GT)
                        if h == 0:
                            act.wait_ge(s_lst, g + 1)
                            A.activation(lns[:, u, LN_SD, :], lns[:, u, LN_VE, :], ACT.Sqrt).then_inc(s_lsd, 1)
                            act.wait_ge(s_lrs, g + 1)
                            relu_rows(P, u, tr[:, s, :], tr[:, s, :], 0, GT)
                            relu_rows(P, u, xr[:, s, :], hr[:, s, :], GT, GT).then_inc(s_lh, 1)
                            act.wait_ge(s_ohT, g + 1)
                            A.copy(ohT[:, :, :], ps[6][:, :, :]).then_inc(s_ohTs, 1)
                            act.wait_ge(s_hT, g + 1)
                            A.copy(hT[:, :, :], ps[4][:, :, :]).then_inc(s_hTs, 1)
                        act.wait_ge(s_rtT, c0 + g + 1)
                        A.copy(rtT[:, s, :], ps[u][:, :, :]).then_inc(s_rtTs, 1)
                        act.wait_ge(s_rg, c0 + g + 1)
                        A.activation(thr[:, s, :], ps[2 + u][:, :, :], ACT.Tanh).then_inc(s_th, 1)
                act.wait_ge(s_exp, h + 1)
                A.activation(seg_x, seg_x, ACT.Exp).then_inc(s_expd, 1)

                def partial_out(i):
                    for u in range(2):
                        act.wait_ge(s_bp, c0 + vec(i, u) + 1)
                        reuse(act, s_bst[u], 16 * (h * NI + i))
                        A.copy(bte[:, u, :, :], ps[u][0:2, :, :]).then_inc(s_be, 1)
                partial_out(0)
                with act.Fori(1, NI) as i:
                    partial_out(i)

                spare = rtr if h < HOPS - 1 else thr

                def squares(i, u):
                    g = vec(i, u)
                    act.wait_ge(s_T, c0 + g + 1)
                    for t in range(GT):
                        A.activation(spare[:, u * GT + t, :], ps[u][:, t, :], ACT.Square, scale=invc[:, bass.ds(g * GT + t, 1)],
                                     accum_out=nrm[:, u, 0, t:t + 1]).then_inc(s_sq, 1)
                    act.wait_ge(s_sq, GT * (c0 + g + 1))
                    A.activation(nrm[:, u, 1, :], nrm[:, u, 0, :], ACT.Sqrt).then_inc(s_nr, 1)

                def evacuate(i, u):
                    g = vec(i, u)
                    act.wait_ge(s_aT, c0 + g + 1)
                    A.copy(tr[:, u * GT:(u + 1) * GT, :], ps[2 + u][:, :, :]).then_inc(s_aTs, 1)
                more = h < HOPS - 1
                squares(0, 0)
                squares(0, 1)
                if more:
                    evacuate(0, 0)
                with act.Fori(1, NI) as i:
                    squares(i, 0)
                    if more:
                        evacuate(i - 1, 1)
                    squares(i, 1)
                    if more:
                        evacuate(i, 0)
                if more:
                    evacuate(NI - 1, 1)

        @block.tensor
        def _(pe):
            T = nc.tensor
            pe.wait_ge(s_const, 5)
            with pe.Fori(0, NPH) as i:
                for way, (kk, vv) in enumerate(((kbuf[0], vbuf), (kT[0], vT))):
                    pe.wait_ge(s_srt, 2 * i + way + 1)
                    for c in range(2):
                        T.transpose(ps[0][:, c, :], kk[:, c * P:(c + 1) * P], ident[:, :])
                        ins = T.transpose(ps[1][:, c, :], vv[:, c * P:(c + 1) * P], ident[:, :])
                    ins.then_inc(s_xp, 1)

            def bank(k):
                return ps[k][:, :, :].rearrange("p n f -> p (n f)")
            pe.wait_ge(s_seg, 1)
            for k in range(2):
                for b in range(2):
                    ins = T.transpose(bank(4)[0:1, k * NT + b * Q:k * NT + (b + 1) * Q], gcol[:, k, b:b + 1], ident[0:Q, 0:Q])
            ins.then_inc(s_segp, 1)

            def to_tiles(k, out_):
                for b in range(2):
                    ins = T.transpose(out_[:, b * Q:(b + 1) * Q], lx[k][:, b, :], ident[0:Q, 0:Q])
                return ins
            pe.wait_ge(s_seg, 2)
            for k in range(7):
                to_tiles(k, bank(k // 2)[:, (k % 2) * NT:(k % 2 + 1) * NT])
            T.matmul(bank(5)[:, 0:2 * NT], onesr[:, :], rows[:, WGF:WGB + 1, :].rearrange("p k n -> p (k n)"), start=True, stop=True)
            T.matmul(bank(6)[:, 0:NT], onesr[:, :], rows[:, G_, :], start=True, stop=True).then_inc(s_segp, 1)

            segs = [2]

            def asked():
                segs[0] += 1
                pe.wait_ge(s_seg, segs[0])

            def whole_segments():
                asked()
                for k, (t, r) in enumerate(((seg_f, R - 1), (seg_b, 0))):
                    for b in range(2):
                        ins = T.transpose(bank(4)[0:1, k * NT + b * Q:k * NT + (b + 1) * Q], t[:, b, r:r + 1], ident[0:Q, 0:Q])
                ins.then_inc(s_segp, 1)
                asked()
                for k in range(2):
                    for b in range(2):
                        ins = T.transpose(bank(4)[0:Q, 400 + 2 * k + b:401 + 2 * k + b], rcar[k][:, b * Q:(b + 1) * Q], ident[0:1, 0:1])
                ins.then_inc(s_segp, 1)

            def weights_to_tiles():
                asked()
                to_tiles(0, bank(0)[:, 0:NT]).then_inc(s_segp, 1)
            whole_segments()
            weights_to_tiles()

            for h in range(HOPS):
                c0 = h * NG
                def rights(i):
                    for u in range(2):
                        g = vec(i, u)
                        if h == 0:
                            pe.wait_ge(s_oh, g + 1)
                            for t in range(GT):
                                ins = T.transpose(ps[6][:, t, :], oh[:, t, :], ident[:, :])
                            ins.then_inc(s_ohT, 1)
                            pe.wait_ge(s_ohTs, g + 1)
                            reuse(pe, s_rele, g)
                            for t in range(GT):
                                ins = T.matmul(ps[7][:, t, :], ohT[:, t, :], emb[:, :], start=True, stop=True)
                            ins.then_inc(s_rel, 1)
                            pe.wait_ge(s_lh, g + 1)
                            for t in range(GT):
                                ins = T.transpose(ps[4][:, t, :], hr[:, u * GT + t, :], ident[:, :])
                            ins.then_inc(s_hT, 1)
                        pe.wait_ge(s_rt, c0 + g + 1)
                        for t in range(GT):
                            ins = T.transpose(ps[u][:, t, :], rtr[:, u * GT + t, :], ident[:, :])
                        ins.then_inc(s_rtT, 1)
                        pe.wait_ge(s_rtTs, c0 + g + 1)
                        for t in range(GT):
                            ins = T.matmul(ps[2 + u][:, t, :], rtT[:, u * GT + t, :], kw[:, :], start=True, stop=True)
                        ins.then_inc(s_rg, 1)
                        if h == 0:
                            pe.wait_ge(s_hTs, g + 1)
                            reuse(pe, s_att, g)
                            for t in range(GT):
                                ins = T.matmul(ps[5][:, t, :], hT[:, t, :], qw[:, :], start=True, stop=True)
                            ins.then_inc(s_left, 1)
                rights(0)
                with pe.Fori(1, NI) as i:
                    rights(i)

                asked()
                for b in range(2):
                    ins = T.transpose(ps[4][0:Q, b, :], att[:, b * Q:(b + 1) * Q], ident[:, :])
                ins.then_inc(s_segp, 1)
                whole_segments()
                whole_segments()
                weights_to_tiles()

                for u in range(2):
                    pe.wait_ge(s_cp[u], 16 * NI * (h + 1))

                def partial(i, u, first=False):
                    g = vec(i, u)
                    pe.wait_ge(s_wf, c0 + g + 1)
                    if not first:
                        pe.wait_ge(s_be, c0 + g - 1)
                    for t in range(GT):
                        ins = T.matmul(ps[u][0:2, t, :], wflr[:, u * GT + t, :],
                                       rt[:, bass.ds(g * GT + t, 1), :].rearrange("p a f -> p (a f)"), start=True, stop=True)
                    ins.then_inc(s_bp, 1)
                partial(0, 0, True)
                partial(0, 1, True)
                with pe.Fori(1, NI) as i:
                    partial(i, 0)
                    partial(i, 1)
                pe.wait_ge(s_rd, 48 + 48 * h + 32)
                for k in range(2):
                    for b in range(2):
                        ins = T.transpose(bank(4)[:, k * NT + b * Q:k * NT + (b + 1) * Q], btr[:, b, k, :], ident[0:Q, 0:Q])
                ins.then_inc(s_part, 1)
                asked()
                for k in range(2):
                    for b in range(2):
                        ins = T.transpose(ps[5][0:Q, 2 * b + k, :], cT[:, k, b * Q:(b + 1) * Q], ident[:, :])
                ins.then_inc(s_segp, 1)
                pe.wait_ge(s_rd, 48 + 48 * (h + 1))

                def sums(i, u, first=False):
                    g = vec(i, u)
                    pe.wait_ge(s_w, c0 + g + 1)
                    if not first:
                        pe.wait_ge(s_ag, c0 + g - 1)
                    for t in range(GT):
                        ins = T.matmul(ps[u][:, t, :], rtT[:, u * GT + t, :],
                                       rt[:, bass.ds(g * GT + t, 1), :].rearrange("p a f -> p (a f)"), start=True, stop=True)
                    ins.then_inc(s_T, 1)

                def turn(i, u):
                    g = vec(i, u)
                    pe.wait_ge(s_ag, c0 + g + 1)
                    for t in range(GT):
                        ins = T.transpose(ps[2 + u][:, t, :], hr[:, u * GT + t, :], ident[:, :])
                    ins.then_inc(s_aT, 1)

                def lefts(i, u, first=False):
                    g = vec(i, u)
                    pe.wait_ge(s_aTs, c0 + g + 1)
                    if not first:
                        pe.wait_ge(s_Le, c0 + g - 1)
                    for t in range(GT):
                        ins = T.matmul(ps[4 + u][:, t, :], tr[:, u * GT + t, :], qw[:, :], start=True, stop=True)
                    ins.then_inc(s_L, 1)
                more = h < HOPS - 1
                sums(0, 0, True)
                sums(0, 1, True)
                if more:
                    turn(0, 0)
                sums(1, 0)
                if more:
                    turn(0, 1)
                    lefts(0, 0, True)
                sums(1, 1)
                if more:
                    turn(1, 0)
                    lefts(0, 1, True)
                with pe.Fori(2, NI) as i:
                    for u in range(2):
                        sums(i, u)
                        if more:
                            turn(i - 1 + u, 1 - u)
                            lefts(i - 1, u)
                if more:
                    turn(NI - 1, 1)
                    lefts(NI - 1, 0)
                    lefts(NI - 1, 1)


_INS = ['x', 'src', 'dst', 'edge_type_64', 'L0_gnn_edge_emb', 'L0_gnn_q_w', 'L0_gnn_k_w']


def kernel(**inputs):
    import numpy as _np
    import concourse.bacc as _bacc
    from concourse import mybir as _mybir
    from concourse.bass_utils import run_bass_kernel_spmd as _run

    nc = _bacc.Bacc("TRN2", target_bir_lowering=False, num_devices=1)
    arrays, args = {}, []
    for name in _INS:
        a = _np.ascontiguousarray(inputs[name])
        arrays[f"in_{name}_dram"] = a
        args.append(nc.dram_tensor(f"in_{name}_dram", a.shape, _mybir.dt.from_np(a.dtype), kind="ExternalInput").ap())
    args.append(nc.dram_tensor("out_0_dram", (50000, 128), _mybir.dt.float32, kind="ExternalOutput").ap())
    gnn_kernel(nc, *args)
    r = _run(nc, [arrays], core_ids=[0])
    return r.results[0]["out_0_dram"]
```

```python
from contextlib import ExitStack

import concourse.bass as bass
from concourse import mybir

F32 = mybir.dt.float32
I32 = mybir.dt.int32
U8 = mybir.dt.uint8
ALU = mybir.AluOpType
ACT = mybir.ActivationFunctionType

N, E, D, NREL = 50000, 25000, 128, 64
HOPS = 3
R = 125
NT = E // R
P = 128
NS = NT * P
Q = NT // 2
GT = 4
NG = NT // GT
NI = NG // 2
TS = 4
NF = NG // TS
SC = 256
LOGN = 15
DR = 125
DK = N // DR
DC = 8
ND = DK // DC
BIG = 3.0e38
EPS = 1e-5
PADKEY = 65536.0
NOSEG = 200.0
NTYPES_PAD = 64.0
LN_SUM, LN_DIF, LN_Q, LN_D2, LN_V, LN_VE, LN_Y, LN_A, LN_RS, LN_NB = range(10)
RSQRT_BITS = 1597463007.0
NPH = LOGN - 8


def gnn_kernel(nc, x, src, dst, etype, edge_emb, q_w, k_w, out):
    ctx = ExitStack()
    with ctx:
        def sb(name, shape, dt=F32):
            return ctx.enter_context(nc.sbuf_tensor(name, shape, dt))

        def sem(name):
            return ctx.enter_context(nc.semaphore(name))

        def dram(name, shape, dt=F32):
            return nc.dram_tensor(name, shape, dt, kind="Internal").ap()

        hs_d = dram("hs_d", [32768 + 128])
        vs_d = dram("vs_d", [32768])
        lid_d = dram("lid_d", [NS], U8)
        ntab_d = dram("ntab_d", [N, D])
        rel_d = dram("rel_d", [NS, D])
        base_d = dram("base_d", [NS, D])
        left_d = [dram(f"left{k}_d", [NS, D]) for k in range(2)]
        agg_d = [dram(f"agg{k}_d", [NS, D]) for k in range(2)]
        bt_d = dram("bt_d", [2, NT * D])
        fx_d = dram("fx_d", [2, NT * D])

        def slots(t):
            return t[0:NS, :].rearrange("(n p) f -> p n f", p=P)

        rt = sb("rt", [P, NT, D])
        segbc = sb("segbc", [P, NT, P], U8)
        tr = sb("tr", [P, TS * GT, D])
        xr = sb("xr", [P, TS * GT, D])
        relr = sb("relr", [P, 2 * GT, D])
        rtr = sb("rtr", [P, 2 * GT, D])
        rtT = sb("rtT", [P, 2 * GT, D])
        thr = sb("thr", [P, 2 * GT, D])
        hr = sb("hr", [P, 2 * GT, D])
        hT = sb("hT", [P, GT, D])
        minus1 = sb("minus1", [1, 1])
        ident = sb("ident", [P, P])
        kw = sb("kw", [D, D])
        qw = sb("qw", [D, D])
        emb = sb("emb", [P, D])
        iota_c = sb("iota_c", [P, P])
        ohT = sb("ohT", [P, GT, P])
        oh = sb("oh", [P, GT, P])
        onesr = sb("onesr", [1, P])
        stats = sb("stats", [P, 2 * GT, 6])
        lns = sb("lns", [P, 2, 10, 2 * GT])
        flat = rt[:, :, :].rearrange("p n f -> p (n f)")
        kbuf = [flat[:, i * SC:(i + 1) * SC] for i in range(2)]
        kT = [flat[:, (2 + i) * SC:(3 + i) * SC] for i in range(2)]
        vbuf = flat[:, 4 * SC:5 * SC]
        vT = flat[:, 5 * SC:6 * SC]
        swapm = flat[:, 6 * SC:6 * SC + 128]
        swapd = flat[:, 7 * SC:7 * SC + 128]
        raws = [flat[:, (8 + i) * SC:(9 + i) * SC].bitcast(I32) for i in range(3)]
        sgn = [flat[:, (11 + i) * SC:(12 + i) * SC] for i in range(8)]
        xd = [xr[0:DR, 2 * GT:4 * GT, :], hr[0:DR, :, :]]
        hd = sb("hd", [DR, DC, D])
        pbits = sb("pbits", [P, 9], I32)
        sgnp = sb("sgnp", [P, 9])
        hp = sb("hp", [Q, 2, R + 2])
        vl = sb("vl", [Q, 2, R])
        vi = sb("vi", [Q, 2, R], I32)
        ti = sb("ti", [Q, 2, R], I32)
        gf = sb("gf", [Q, 2, R])
        gb = sb("gb", [Q, 2, R])
        gfn = sb("gfn", [Q, 2, R])
        gbn = sb("gbn", [Q, 2, R])
        def lin(ring, k, w):
            return ring[0:Q, 0:2 * GT, :].rearrange("p n f -> p (n f)")[:, k * 2 * P:k * 2 * P + 2 * w].rearrange("p (b r) -> p b r", b=2)
        seg_x, seg_xf, seg_xb, seg_f = (lin(tr, k, R) for k in range(4))
        seg_b = lin(xr, 0, R)
        lx = [lin(xr, k, P) for k in range(1, 4)] + [lin(relr, k, P) for k in range(4)]
        LH, LT, LS, LY, LL, LF, LB = range(7)
        lid8 = sb("lid8", [Q, 2, P], U8)
        gcol = sb("gcol", [Q, 2, 2])
        rows = sb("rows", [1, 8, NT])
        G_, GN, WGF, WGB, GNEG, GNNEG, WGFN, WGBN = range(8)
        thrf = thr[0:1, :, :].rearrange("p n f -> p (n f)")
        hrf = hr[0:1, :, :].rearrange("p n f -> p (n f)")
        whrow = thrf[:, 0:NT]
        rscan = [thrf[:, (1 + k) * NT:(2 + k) * NT] for k in range(2)]
        rcar = [hrf[:, k * NT:(k + 1) * NT] for k in range(2)]
        lcol = sb("lcol", [P, NT])
        hidx = sb("hidx", [P, NT], I32)
        tidx = sb("tidx", [P, NT], I32)
        lidx = sb("lidx", [P, NT], I32)
        tycol = sb("tycol", [P, NT])
        mfl = sb("mfl", [P, 2, NT])
        invc = sb("invc", [P, NT])
        att = sb("att", [P, NT])
        wcol = sb("wcol", [P, NT])
        wfl = sb("wfl", [P, NT, 2])
        wflr = sb("wflr", [P, 2 * GT, 2])
        bcg = sb("bcg", [P, 3, NT])
        scT = relr[:, :, :].rearrange("p n f -> p (n f)")[:, 0:2 * NT].rearrange("p (k n) -> p k n", k=2)
        cT = tr[:, :, :].rearrange("p n f -> p (n f)")[:, 0:2 * NT].rearrange("p (k n) -> p k n", k=2)
        attr = sb("attr", [P, 2, GT])
        nrm = sb("nrm", [P, 2, 4, GT])
        stg = sb("stg", [P, TS, GT], I32)
        stg2 = sb("stg2", [P, TS, GT], I32)
        btr = hr[0:Q, 0:4, :].rearrange("p (b k) f -> p b k f", b=2)
        fxr = hr[0:Q, 4:8, :].rearrange("p (b k) f -> p b k f", b=2)
        bte = thr[0:2, :, :].rearrange("a (u t) f -> a u t f", u=2)

        ps = [ctx.enter_context(nc.psum_tensor(f"ps{i}", [P, GT, D], F32)) for i in range(8)]

        s_ld = sem("s_ld")
        s_const = sem("s_const")
        s_dve = sem("s_dve")
        s_srt = sem("s_srt")
        s_part = sem("s_part")
        s_sq = sem("s_sq")
        s_xp = sem("s_xp")
        s_seg = sem("s_seg")
        s_segp = sem("s_segp")
        s_exp = sem("s_exp")
        s_expd = sem("s_expd")
        s_wr = sem("s_wr")
        s_rd = sem("s_rd")
        s_go = sem("s_go")
        s_z = sem("s_z")
        s_xd = [sem(f"s_xd{u}") for u in range(2)]
        s_od = [sem(f"s_od{u}") for u in range(2)]
        s_dln = sem("s_dln")
        s_dh = sem("s_dh")
        s_do = sem("s_do")
        s_t = [sem(f"s_t{u}") for u in range(TS)]
        s_rl = [sem(f"s_rl{u}") for u in range(2)]
        s_cp = [sem(f"s_cp{u}") for u in range(2)]
        s_bs = [sem(f"s_bs{u}") for u in range(2)]
        s_rt = sem("s_rt")
        s_att = sem("s_att")
        s_rtT = sem("s_rtT")
        s_rtTs = sem("s_rtTs")
        s_rg = sem("s_rg")
        s_th = sem("s_th")
        s_ln = sem("s_ln")
        s_lh = sem("s_lh")
        s_oh = sem("s_oh")
        s_ohT = sem("s_ohT")
        s_ohTs = sem("s_ohTs")
        s_rel = sem("s_rel")
        s_rele = sem("s_rele")
        s_base = sem("s_base")
        s_hT = sem("s_hT")
        s_hTs = sem("s_hTs")
        s_left = sem("s_left")
        s_wf = sem("s_wf")
        s_bp = sem("s_bp")
        s_be = sem("s_be")
        s_bst = [sem(f"s_bst{u}") for u in range(2)]
        s_w = sem("s_w")
        s_T = sem("s_T")
        s_nr = sem("s_nr")
        s_ag = sem("s_ag")
        s_agst = [sem(f"s_agst{u}") for u in range(2)]
        s_aT = sem("s_aT")
        s_aTs = sem("s_aTs")
        s_L = sem("s_L")
        s_Le = sem("s_Le")
        s_Lst = [sem(f"s_Lst{u}") for u in range(2)]
        s_fl = [sem(f"s_fl{u}") for u in range(2)]
        s_fin = sem("s_fin")
        s_sc = [sem(f"s_sc{u}") for u in range(2)]
        s_zero = sem("s_zero")
        s_hop = sem("s_hop")
        s_pace = sem("s_pace")
        s_pool = sem("s_pool")
        s_fix = sem("s_fix")

        PADROWS = (E // SC, E % SC)
        LOADS = 0
        def runs(t):
            return t.rearrange("(p n) f -> p n f", p=DR)
        block = ctx.enter_context(nc.Block())

        class Group:

            def __init__(self, i, r):
                self.i, self.slot = (i + r // TS if r // TS else i), r % TS
                self.g = self.i * TS + self.slot
                self.u = self.slot % 2
                self.nth = self.i * 2 + self.slot // 2
                self.tiles = bass.ds(self.g * GT, GT)
                self.ring = slice(self.u * GT, (self.u + 1) * GT)
                self.ring4 = slice(self.slot * GT, (self.slot + 1) * GT)

            def back(self, k):
                return Group(self.i, self.slot - k)

            def tile(self, t):
                return bass.ds(self.g * GT + t, 1)

            def exists(self, k=0):
                return not isinstance(self.g, int) or 0 <= self.g + k < NG

        def groups(eng, step, lag=0, chain=None):
            for i in range(2):
                if chain is not None:
                    before = chain.at
                for r in range(TS):
                    step(Group(i, r))
            if chain is not None:
                start, per = before, chain.at - before
            with eng.Fori(2, NF) as i:
                if chain is not None:
                    chain.at = start + (i - 1) * per
                for r in range(TS):
                    step(Group(i, r))
            if chain is not None:
                chain.at = start + (NF - 1) * per
            for r in range(NG % TS + lag):
                step(Group(NF, r))

        def chunk(h, n):
            k = (h - 1) * NI + n.slot // 2
            return k + n.i * 2, k % 2, k // 2 + n.i

        def stored(h, w):
            return (h * NI + 1 - w) // 2

        def vec(i, u):
            return 2 * i + u

        def reuse(eng, sem_, value):
            if not isinstance(value, int) or value > 0:
                eng.wait_ge(sem_, value)

        N_BIDIR = 2
        SETUP_SEG = 2 + N_BIDIR + 1 + 1

        @block.sync
        def _(sp):
            whole, rest = PADROWS
            sp.wait_ge(s_zero, 1)
            for t, a in zip(raws, (src, dst, etype)):
                sp.dma_start(t[0:whole, :], a[0:whole * SC].rearrange("(p c) -> p c", c=SC)).then_inc(s_ld, 16)
                sp.dma_start(t[whole:whole + 1, 0:rest], a[whole * SC:E].rearrange("(p c) -> p c", p=1)).then_inc(s_ld, 16)
            sp.dma_start(kw[:, :], k_w[:, :]).then_inc(s_ld, 16)
            sp.dma_start(qw[:, :], q_w[:, :]).then_inc(s_ld, 16)
            sp.dma_start(emb[0:NREL, :], edge_emb[:, :]).then_inc(s_ld, 16)
            with sp.Fori(0, ND) as i:
                sp.dma_start(runs(ntab_d)[:, bass.ds(i * DC, DC), :], rtT[0:DR, :, :]).then_inc(s_z, 16)

            sp.wait_ge(s_go, 1)
            sp.dma_start(hs_d[0:1].rearrange("(a b) -> a b", a=1), minus1[:, :]).then_inc(s_wr, 16)
            sp.dma_start(hs_d[1:32769].rearrange("(p c) -> p c", c=SC), kbuf[0]).then_inc(s_wr, 16)
            sp.dma_start(vs_d.rearrange("(p c) -> p c", c=SC), vbuf).then_inc(s_wr, 16)
            sp.wait_ge(s_wr, 48)
            hs_v = bass.AP(tensor=hs_d.tensor, offset=0, ap=[[R, Q], [R * Q, 2], [1, R + 2]])
            sp.dma_start(hp[:, :, :], hs_v).then_inc(s_rd, 16)
            sp.dma_start(vl[:, :, :], vs_d[0:E].rearrange("(b q r) -> q b r", b=2, r=R)).then_inc(s_rd, 16)
            sp.wait_ge(s_go, 2)
            sp.dma_start(lid_d.rearrange("(b q r) -> q b r", b=2, r=P), lid8[:, :, :]).then_inc(s_wr, 16)
            sp.wait_ge(s_wr, 64)
            sp.dma_start(segbc[:, :, :].rearrange("p n f -> p (n f)"),
                         lid_d[:].rearrange("(a b) -> a b", a=1).broadcast_to([P, NS])).then_inc(s_rd, 16)

            wr, rd = 64, 48
            for h in range(HOPS):
                c0 = h * NG
                def load_rl(n):
                    sp.dma_start(relr[:, n.ring, :], slots(rel_d)[:, n.tiles, :]).then_inc(s_rl[n.u], 16)
                    sp.dma_start(xr[:, n.ring, :], slots(left_d[h - 1])[:, n.tiles, :]).then_inc(s_rl[n.u], 16)

                def load_x(n):
                    c, w, nth = chunk(h, n)
                    sp.dma_start(xd[w], runs(x)[:, bass.ds(c * DC, DC), :]).then_inc(s_xd[w], 16)

                def edges(n):
                    sp.wait_ge(s_rt, c0 + n.g + 1)
                    sp.dma_start(rt[:, n.tiles, :], rtr[:, n.ring, :]).then_inc(s_cp[n.u], 16)
                    if h == 0:
                        sp.dma_start(slots(rel_d)[:, n.tiles, :], relr[:, n.ring, :]).then_inc(s_bs[n.u], 16)
                        sp.dma_start(slots(base_d)[:, n.tiles, :], xr[:, n.ring4, :]).then_inc(s_bs[n.u], 16)
                        return
                    if n.exists(2):
                        sp.wait_ge(s_att, c0 + n.g + 1)
                        load_rl(n.back(-2))
                    if n.u == 1:
                        c, w, nth = chunk(h, n)
                        sp.wait_ge(s_do, c + 1)
                        sp.dma_start(runs(out)[:, bass.ds(c * DC, DC), :], xd[w]).then_inc(s_od[w], 16)
                        if n.back(2).exists() and n.exists(2):
                            c, w, nth = chunk(h, n.back(2))
                            sp.wait_ge(s_od[w], 16 * (nth + 1))
                            load_x(n.back(-2))
                if h > 0:
                    load_rl(Group(0, 0))
                    load_rl(Group(0, 1))
                    for u in range(2):
                        sp.wait_ge(s_sc[u], 16 * GT * NI * h)
                        reuse(sp, s_od[u], 16 * stored(h - 1, u))
                    load_x(Group(0, 1))
                    load_x(Group(0, 3))
                groups(sp, edges)
                if h == 0:
                    for u in range(2):
                        sp.wait_ge(s_bs[u], 32 * NI)
                with sp.Fori(0, NI) as i:
                    for u in range(2):
                        g = vec(i, u)
                        sp.wait_ge(s_be, c0 + g + 1)
                        sp.dma_start(bt_d[:, bass.ds(g * GT * D, GT * D)], bte[:, u, :, :].rearrange("a t f -> a (t f)")).then_inc(s_bst[u], 16)
                for u in range(2):
                    sp.wait_ge(s_bst[u], 16 * NI * (h + 1))
                for k in range(2):
                    sp.dma_start(btr[:, :, k, :], bt_d[k, :].rearrange("(b q f) -> q b f", b=2, f=D)).then_inc(s_rd, 16)
                rd += 32
                sp.wait_ge(s_fix, h + 1)
                for k in range(2):
                    sp.dma_start(fx_d[k, :].rearrange("(b q f) -> q b f", b=2, f=D), fxr[:, :, k, :]).then_inc(s_wr, 16)
                wr += 32
                sp.wait_ge(s_wr, wr)
                sp.dma_start(rt[R:R + 2, :, :].rearrange("a n f -> a (n f)"), fx_d[:, :]).then_inc(s_rd, 16)
                rd += 16

                if h < HOPS - 1:
                    def results(n):
                        if n.exists():
                            sp.wait_ge(s_ag, c0 + n.g + 1)
                            sp.dma_start(slots(agg_d[h])[:, n.tiles, :], hr[:, n.ring, :]).then_inc(s_agst[n.u], 16)
                        m = n.back(2)
                        if m.exists():
                            sp.wait_ge(s_Le, c0 + m.g + 1)
                            sp.dma_start(slots(left_d[h])[:, m.tiles, :], thr[:, m.ring, :]).then_inc(s_Lst[m.u], 16)
                    groups(sp, results, lag=2)
                    for u in range(2):
                        sp.wait_ge(s_agst[u], 16 * NI * (h + 1))
                        sp.wait_ge(s_Lst[u], 16 * NI * (h + 1))
                else:
                    def load_final(n):
                        m = n.back(2)
                        if m.exists():
                            sp.wait_ge(s_fin, m.g + 1)
                        if n.exists():
                            for t, d in ((tr, base_d), (xr, agg_d[0]), (relr, agg_d[1])):
                                sp.dma_start(t[:, n.ring, :], slots(d)[:, n.tiles, :]).then_inc(s_fl[n.u], 16)
                    groups(sp, load_final)
            for u in range(2):
                sp.wait_ge(s_sc[u], HOPS * 16 * GT * NI)
                sp.wait_ge(s_od[u], 16 * (ND // 2))
                sp.wait_ge(s_bs[u], 32 * NI)

        @block.gpsimd
        def _(pool):
            def pool_wait(sem_, value):
                pool.wait_ge(sem_, value)
                pool.sem_inc(s_pace, 1)

            def reuse_pool(sem_, value):
                if not isinstance(value, int) or value > 0:
                    pool_wait(sem_, value)
            nc.gpsimd.iota(iota_c[:, :], pattern=[[1, P]], base=0, channel_multiplier=0,
                           allow_small_or_imprecise_dtypes=True).then_inc(s_const, 1)
            nc.gpsimd.memset(ident[:, :], 1.0).then_inc(s_const, 1)
            pool.wait_ge(s_const, 2)
            nc.gpsimd.affine_select(ident[:, :], ident[:, :], pattern=[[1, P]], base=0, channel_multiplier=-1,
                                    compare_op=ALU.is_equal, fill=0.0).then_inc(s_const, 1)
            for k in range(1, 8):
                nc.gpsimd.iota(sgn[k], pattern=[[0, SC >> (k + 1)], [-2, 2], [0, 1 << k]], base=1, channel_multiplier=0,
                               allow_small_or_imprecise_dtypes=True).then_inc(s_const, 1)
            nc.gpsimd.iota(pbits[:, 8:9], pattern=[[0, 1]], base=0, channel_multiplier=1).then_inc(s_const, 1)

            pool.wait_ge(s_go, 4)

            staged = [0, 0]

            def staging(n, k):
                return staged[0] + n.g * staged[1] + k

            def scatter(n, table, rows):
                for t in range(GT):
                    nc.gpsimd.indirect_dma_start(out=table[:, :], out_offset=bass.IndirectOffsetOnAxis(ap=stg[:, n.slot, t:t + 1], axis=0),
                                                 in_=rows[:, n.u * GT + t, :], in_offset=None, bounds_check=N - 1,
                                                 oob_is_err=False).then_inc(s_sc[n.u], 16)

            for h in range(HOPS):
                c0 = h * NG

                def fetch(n):
                    if h == 0:
                        m = n.back(TS)
                        if m.exists():
                            pool_wait(s_rt, m.g + 1)
                            pool_wait(s_bs[m.u], 32 * (m.nth + 1))
                    else:
                        pool_wait(s_rt, c0 - TS + n.g + 1)
                    nc.gpsimd.tensor_copy(stg[:, n.slot, :], tidx[:, n.tiles]).then_inc(s_pool, 1)
                    if h == 0:
                        nc.gpsimd.tensor_copy(stg2[:, n.slot, :], hidx[:, n.tiles]).then_inc(s_pool, 1)
                    pool_wait(s_pool, staging(n, staged[1]))
                    for t in range(GT):
                        k = n.slot * GT + t
                        nc.gpsimd.indirect_dma_start(out=tr[:, k, :], out_offset=None, in_=(x if h == 0 else ntab_d)[:, :],
                                                     in_offset=bass.IndirectOffsetOnAxis(ap=stg[:, n.slot, t:t + 1], axis=0)).then_inc(s_t[n.slot], 16)
                        if h == 0:
                            nc.gpsimd.indirect_dma_start(out=xr[:, k, :], out_offset=None, in_=x[:, :],
                                                         in_offset=bass.IndirectOffsetOnAxis(ap=stg2[:, n.slot, t:t + 1], axis=0)).then_inc(s_t[n.slot], 16)
                if h > 0:
                    for u in range(2):
                        pool.wait_ge(s_sc[u], 16 * GT * NI * h)
                    pool.wait_ge(s_Le, NG * h)
                staged[1] = 2 if h == 0 else 1
                groups(pool, fetch)
                staged[0] += NG * staged[1]

                if h == 0:
                    pool.wait_ge(s_z, 16 * ND)
                pool.wait_ge(s_rt, c0 + NG)
                if h == HOPS - 1:
                    for u in range(2):
                        pool.wait_ge(s_od[u], 16 * (ND // 2))
                staged[1] = 1

                def put(n):
                    m = n.back(TS)
                    if m.exists():
                        pool_wait(s_sc[m.u], 16 * GT * (h * NI + m.nth + 1))
                    nc.gpsimd.tensor_copy(stg[:, n.slot, :], lidx[:, n.tiles]).then_inc(s_pool, 1)
                    pool_wait(s_pool, staging(n, 1))
                    if h < HOPS - 1:
                        pool_wait(s_ag, c0 + n.g + 1)
                        scatter(n, ntab_d, hr)
                    else:
                        pool_wait(s_fin, n.g + 1)
                        scatter(n, out, rtr)
                groups(pool, put)
                staged[0] += NG

        @block.vector
        def _(dve):
            V = nc.vector

            class Chain:
                at = 0

                def note(self, ins):
                    self.at = self.at + 1
                    ins.then_inc(s_dve, 1)

                def join(self):
                    dve.wait_ge(s_dve, self.at)

                def __call__(self, ins):
                    self.note(ins)
                    self.join()
            ch = Chain()

            ch.note(V.memset(minus1[:, :], -1.0))
            ch.note(V.memset(onesr[:, :], 1.0))
            ch.note(V.memset(raws[0], int(PADKEY)))
            ch.note(V.memset(raws[1], 0))
            ch.note(V.memset(raws[2], 0))
            ch.note(V.memset(emb[:, :], 0.0))
            ch(V.memset(rtT[:, :, :], 0.0))
            dve.sem_inc(s_zero, 1)

            def layer_norm(pr, u, n, s_out):
                def L(k):
                    return lns[0:pr, u, k, 0:n]
                me, qe, mo, qo = (stats[0:pr, 0:n, k] for k in (1, 2, 4, 5))
                ch.note(V.tensor_tensor(L(LN_SUM), me, mo, ALU.add))
                ch.note(V.tensor_tensor(L(LN_DIF), me, mo, ALU.subtract))
                ch(V.tensor_tensor(L(LN_Q), qe, qo, ALU.add))
                ch(V.tensor_tensor(L(LN_D2), L(LN_DIF), L(LN_DIF), ALU.mult))
                ch(V.scalar_tensor_tensor(L(LN_V), L(LN_D2), D / 4.0, L(LN_Q), ALU.mult, ALU.add))
                ch(V.tensor_scalar(L(LN_VE), L(LN_V), 1.0 / D, EPS, ALU.mult, ALU.add))
                ch(V.tensor_scalar(L(LN_Y).bitcast(I32), L(LN_VE).bitcast(I32), -0.5, RSQRT_BITS, ALU.mult, ALU.add))
                y = LN_Y
                for k in range(3):
                    to = LN_RS if y == LN_Y else LN_Y
                    ch(V.scalar_tensor_tensor(L(LN_A), L(y), -0.5, L(y), ALU.mult, ALU.mult))
                    ch(V.tensor_tensor(L(LN_A), L(LN_A), L(LN_VE), ALU.mult))
                    ch(V.scalar_tensor_tensor(L(to), L(LN_A), 1.5, L(y), ALU.add, ALU.mult))
                    y = to
                V.scalar_tensor_tensor(L(LN_NB), L(LN_SUM), -0.5, L(LN_RS), ALU.mult, ALU.mult).then_inc(s_out, 1)

            def dense_in(h, n):
                c, w, nth = chunk(h, n)
                dve.wait_ge(s_xd[w], 16 * (nth + 1))
                for t in range(DC):
                    ch.note(V.bn_stats(stats[0:DR, t, :], xd[w][:, t, :]))
                ch.join()
                layer_norm(DR, 0, DC, s_dln)

            def dense_out(h, n):
                c, w, nth = chunk(h, n)
                dve.wait_ge(s_dh, c + 1)
                V.scalar_tensor_tensor(xd[w].rearrange("p n f -> p (n f)"), hd[:, :, :].rearrange("p n f -> p (n f)"), 3.0,
                                       xd[w].rearrange("p n f -> p (n f)"), ALU.mult, ALU.add).then_inc(s_do, 1)

            dve.wait_ge(s_ld, 16 * 9)
            ch.note(V.tensor_copy(kbuf[0], raws[0]))
            ch.note(V.scalar_tensor_tensor(vbuf, raws[1], float(NREL), raws[2], ALU.mult, ALU.add))
            dve.wait_ge(s_const, 11)
            for k in range(8):
                ch.note(V.tensor_scalar(pbits[:, k:k + 1], pbits[:, 8:9], k, 1, ALU.logical_shift_right, ALU.bitwise_and))
            ch.join()
            ch(V.tensor_scalar(sgnp[:, 0:8], pbits[:, 0:8], -2.0, 1.0, ALU.mult, ALU.add))

            def exchange(a_buf, b_buf, v, stride):
                def halves(t):
                    w = t.rearrange("p (n t s) -> p n t s", t=2, s=stride)
                    return w[:, :, 0, :], w[:, :, 1, :]
                ka, kb = halves(a_buf)
                na, nb = halves(b_buf)
                va, vb = halves(v)
                m = swapm.rearrange("p (n s) -> p n s", s=stride)
                d = swapd.rearrange("p (n s) -> p n s", s=stride)
                ch.note(V.tensor_tensor(m, ka, kb, ALU.is_gt))
                ch.note(V.tensor_tensor(d, vb, va, ALU.subtract))
                ch.note(V.tensor_tensor(na, ka, kb, ALU.min))
                dve.wait_ge(s_dve, ch.at - 1)
                ch.note(V.tensor_tensor(d, d, m, ALU.mult))
                ch.note(V.tensor_tensor(nb, ka, kb, ALU.max))
                dve.wait_ge(s_dve, ch.at - 1)
                ch.note(V.tensor_tensor(va, va, d, ALU.add))
                ch(V.tensor_tensor(vb, vb, d, ALU.subtract))

            def apply_sign(t, k):
                if 1 <= k < 8:
                    ch(V.tensor_tensor(t, t, sgn[k], ALU.mult))
                elif 8 <= k < LOGN:
                    ch(V.tensor_scalar(t, t, sgnp[:, k - 8:k - 7], None, ALU.mult))

            at, hand = 0, 0
            for k in range(1, LOGN + 1):
                apply_sign(kbuf[at], k - 1)
                apply_sign(kbuf[at], k)
                if k > 8:
                    dve.sem_inc(s_srt, 1)
                    hand += 1
                    dve.wait_ge(s_xp, hand)
                    bt = (k - 8) % 2
                    ch.note(V.tensor_copy(kT[bt], ps[0][:, 0:2, :].rearrange("p n f -> p (n f)")))
                    ch(V.tensor_copy(vT, ps[1][:, 0:2, :].rearrange("p n f -> p (n f)")))
                    for m in range(k - 1, 7, -1):
                        exchange(kT[bt], kT[1 - bt], vT, 1 << (m - 8))
                        bt = 1 - bt
                    dve.sem_inc(s_srt, 1)
                    hand += 1
                    dve.wait_ge(s_xp, hand)
                    ch.note(V.tensor_copy(kbuf[0], ps[0][:, 0:2, :].rearrange("p n f -> p (n f)")))
                    ch(V.tensor_copy(vbuf, ps[1][:, 0:2, :].rearrange("p n f -> p (n f)")))
                for m in range(min(k, 8) - 1, -1, -1):
                    exchange(kbuf[at], kbuf[1 - at], vbuf, 1 << m)
                    at = 1 - at
            assert at == 0
            dve.sem_inc(s_go, 1)

            dve.wait_ge(s_rd, 32)
            cur, first, last_ = hp[:, :, 1:R + 1], hp[:, :, 1:2], hp[:, :, R:R + 1]
            ch.note(V.tensor_tensor(gf[:, :, :], hp[:, :, 0:R], cur, ALU.is_equal))
            ch.note(V.tensor_tensor(gb[:, :, :], hp[:, :, 2:R + 2], cur, ALU.is_equal))
            ch(V.tensor_copy(vi[:, :, :], vl[:, :, :]))
            ch.note(V.tensor_copy(gcol[:, 0, :], gf[:, :, 0:1].rearrange("p b o -> p (b o)")))
            V.tensor_tensor(gcol[:, 1, :], first.rearrange("p b o -> p (b o)"), last_.rearrange("p b o -> p (b o)"),
                            ALU.is_equal).then_inc(s_seg, 1)
            ch.note(V.scalar_tensor_tensor(lx[LL][:, :, 0:R], gb[:, :, :], PADKEY, cur, ALU.mult, ALU.add))
            ch.note(V.memset(lx[LL][:, :, R:P], PADKEY))
            ch.note(V.tensor_copy(lx[LH][:, :, 0:R], cur))
            ch.note(V.memset(lx[LH][:, :, R:P], 0.0))
            ch.note(V.memset(lx[LT][:, :, R:P], 0.0))
            ch.note(V.memset(lx[LY][:, :, R:P], NTYPES_PAD))
            ch.note(V.tensor_tensor(lx[LF][:, :, 0:R], cur, first.to_broadcast([Q, 2, R]), ALU.is_equal))
            ch.note(V.tensor_tensor(lx[LB][:, :, 0:R], cur, last_.to_broadcast([Q, 2, R]), ALU.is_equal))
            ch.note(V.memset(lx[LF][:, :, R:P], 0.0))
            ch.note(V.memset(lx[LB][:, :, R:P], 0.0))
            ch.note(V.tensor_scalar(ti[:, :, :], vi[:, :, :], 6, None, ALU.logical_shift_right))
            ch(V.tensor_scalar(vi[:, :, :], vi[:, :, :], NREL - 1, None, ALU.bitwise_and))
            ch.note(V.tensor_copy(lx[LT][:, :, 0:R], ti[:, :, :]))
            ch.note(V.tensor_copy(lx[LY][:, :, 0:R], vi[:, :, :]))
            ch.note(V.tensor_scalar(seg_x, gf[:, :, :], -1.0, 1.0, ALU.mult, ALU.add))
            ch(V.memset(seg_xf, 1.0))
            ch.note(V.memset(seg_x[:, :, 0:1], 0.0))
            ch.note(V.memset(seg_xf[:, :, 0:1], 0.0))
            ch.note(V.memset(gf[:, :, 0:1], 0.0))
            ch(V.memset(gb[:, :, R - 1:R], 0.0))
            flat2 = "p b r -> p (b r)"
            ch(V.tensor_tensor_scan(seg_f.rearrange(flat2), seg_xf.rearrange(flat2), seg_x.rearrange(flat2), 0.0, ALU.mult, ALU.add))
            ch.note(V.tensor_copy(lx[LS][:, :, 0:R], seg_f))
            ch.note(V.memset(lx[LS][:, :, R:R + 1], 0.0))
            ch.note(V.tensor_copy(lx[LS][:, :, R + 1:R + 2], seg_f[:, :, R - 1:R]))
            ch.note(V.memset(lx[LS][:, :, R + 2:P], NOSEG))
            ch.note(V.tensor_scalar(gfn[:, :, :], gf[:, :, :], BIG, -BIG, ALU.mult, ALU.add))
            ch(V.tensor_scalar(gbn[:, :, :], gb[:, :, :], BIG, -BIG, ALU.mult, ALU.add))
            V.tensor_copy(lid8[:, :, :], lx[LS]).then_inc(s_go, 1)
            dve.wait_ge(s_segp, 1)
            row = ps[4][0:1, :, :].rearrange("p n f -> p (n f)")
            ch.note(V.tensor_copy(rows[:, G_, :], row[:, 0:NT]))
            ch(V.tensor_copy(whrow, row[:, NT:2 * NT]))
            ch.note(V.tensor_copy(rows[:, GN, 0:NT - 1], rows[:, G_, 1:NT]))
            ch(V.memset(rows[:, GN, NT - 1:NT], 0.0))
            ch.note(V.tensor_tensor(rows[:, WGF, :], rows[:, G_, :], whrow, ALU.mult))
            ch(V.tensor_tensor(rows[:, WGB, :], rows[:, GN, :], whrow, ALU.mult))
            for a, b in ((G_, GNEG), (GN, GNNEG), (WGF, WGFN), (WGB, WGBN)):
                ch.note(V.tensor_scalar(rows[:, b, :], rows[:, a, :], BIG, -BIG, ALU.mult, ALU.add))
            ch.join()
            dve.sem_inc(s_seg, 1)
            dve.wait_ge(s_segp, 2)

            def tile_of(k):
                return ps[k // 2][:, :, :].rearrange("p n f -> p (n f)")[:, (k % 2) * NT:(k % 2 + 1) * NT]
            ch.note(V.tensor_copy(hidx[:, :], tile_of(LH)))
            ch.note(V.tensor_copy(tidx[:, :], tile_of(LT)))
            ch.note(V.tensor_copy(lcol[:, :], tile_of(LS)))
            ch.note(V.tensor_copy(tycol[:, :], tile_of(LY)))
            ch.note(V.tensor_copy(lidx[:, :], tile_of(LL)))
            ch.note(V.tensor_copy(mfl[:, 0, :], tile_of(LF)))
            ch.note(V.tensor_copy(mfl[:, 1, :], tile_of(LB)))
            ch.note(V.tensor_copy(bcg[:, 0:2, :], ps[5][:, :, :].rearrange("p n f -> p (n f)")[:, 0:2 * NT].rearrange("p (k n) -> p k n", k=2)))
            ch(V.tensor_copy(bcg[:, 2, :], ps[6][:, :, :].rearrange("p n f -> p (n f)")[:, 0:NT]))
            dve.sem_inc(s_go, 1)

            segs = [2]

            def to_pe():
                dve.sem_inc(s_seg, 1)
                segs[0] += 1
                dve.wait_ge(s_segp, segs[0])

            def whole_segments(add, xin):
                op0, op1 = (ALU.mult, ALU.add) if add else (ALU.add, ALU.max)
                GFt, GBt = (gf, gb) if add else (gfn, gbn)
                rg, rgn, rwf, rwb = (G_, GN, WGF, WGB) if add else (GNEG, GNNEG, WGFN, WGBN)
                none = 0.0 if add else -BIG
                fl, bl = (lambda t: t.rearrange(flat2)), (lambda t: t.rearrange(flat2)[:, ::-1])
                ch.note(V.tensor_copy(seg_xf, xin))
                ch.note(V.tensor_copy(seg_xb, xin))
                ch.note(V.tensor_tensor_scan(fl(seg_f), fl(GFt[:, :, :]), fl(xin), none, op0, op1))
                ch(V.tensor_tensor_scan(bl(seg_b), bl(GBt[:, :, :]), bl(xin), none, op0, op1))
                to_pe()
                ch.note(V.tensor_tensor_scan(rscan[0], rows[:, rwf, :], row[:, 0:NT], none, op0, op1))
                ch.note(V.tensor_tensor_scan(rscan[1][:, ::-1], rows[:, rwb, ::-1], row[:, NT:2 * NT][:, ::-1], none, op0, op1))
                ch.note(V.memset(rcar[0][:, 0:1], none))
                ch.note(V.memset(rcar[1][:, NT - 1:NT], none))
                ch.join()
                ch.note(V.tensor_tensor(rcar[0][:, 1:NT], rows[:, rg, 1:NT], rscan[0][:, 0:NT - 1], op0))
                ch(V.tensor_tensor(rcar[1][:, 0:NT - 1], rows[:, rgn, 0:NT - 1], rscan[1][:, 1:NT], op0))
                to_pe()
                car = ps[4][0:Q, :, :].rearrange("p n f -> p (n f)")
                ch.note(V.tensor_tensor(seg_xf[:, :, 0], xin[:, :, 0], car[:, 400:402], op1))
                ch(V.tensor_tensor(seg_xb[:, :, R - 1], xin[:, :, R - 1], car[:, 402:404], op1))
                ch.note(V.tensor_tensor_scan(fl(seg_f), fl(GFt[:, :, :]), fl(seg_xf), none, op0, op1))
                ch(V.tensor_tensor_scan(bl(seg_b), bl(GBt[:, :, :]), bl(seg_xb), none, op0, op1))
                ch(V.tensor_tensor(seg_f, seg_f, seg_b, op1))
                if add:
                    ch(V.tensor_tensor(seg_f, seg_f, xin, ALU.subtract))

            ch(V.memset(seg_x, 1.0))
            whole_segments(True, seg_x)
            ch(V.tensor_scalar(seg_f, seg_f, 1.0, None, ALU.max))
            ch.note(V.reciprocal(lx[0][:, :, 0:R], seg_f))
            ch(V.memset(lx[0][:, :, R:P], 1.0))
            to_pe()
            ch(V.tensor_copy(invc[:, :], ps[0][:, :, :].rearrange("p n f -> p (n f)")[:, 0:NT]))
            dve.sem_inc(s_go, 1)

            for h in range(HOPS):
                c0 = h * NG
                tb = [(h + 1) * GT * 16 * (NF + (r < NG % TS)) for r in range(TS)]

                f = "p n f -> p (n f)"

                def norms(n):
                    dve.wait_ge(s_t[n.slot], 2 * GT * 16 * (n.i + 1))
                    for t in range(GT):
                        ch.note(V.bn_stats(stats[:, t, :], tr[:, n.slot * GT + t, :]))
                        ch.note(V.bn_stats(stats[:, GT + t, :], xr[:, n.slot * GT + t, :]))
                    ch.join()
                    layer_norm(P, n.u, 2 * GT, s_ln)
                    reuse(dve, s_ohT, n.g)
                    for t in range(GT):
                        ins = V.tensor_scalar(oh[:, t, :], iota_c[:, :], tycol[:, n.tile(t)], None, ALU.is_equal)
                    ins.then_inc(s_oh, 1)

                def products(n):
                    if h == 0:
                        dve.wait_ge(s_lh, n.g + 1)
                        ch.note(V.scalar_tensor_tensor(xr[:, n.ring4, :].rearrange(f), hr[:, n.ring, :].rearrange(f), 3.0,
                                                       xr[:, n.ring4, :].rearrange(f), ALU.mult, ALU.add))
                        dve.wait_ge(s_rel, n.g + 1)
                        reuse(dve, s_bs[n.u], 32 * n.nth)
                        V.tensor_copy(relr[:, n.ring, :], ps[7][:, :, :]).then_inc(s_rele, 1)
                        dve.wait_ge(s_rele, n.g + 1)
                    else:
                        dve.wait_ge(s_t[n.slot], tb[n.slot] + GT * 16 * (n.i + 1))
                        dve.wait_ge(s_rl[n.u], 32 * ((h - 1) * NI + n.nth + 1))
                    reuse(dve, s_cp[n.u], 16 * (h * NI + n.nth))
                    V.tensor_tensor(rtr[:, n.ring, :], tr[:, n.ring4, :], relr[:, n.ring, :], ALU.mult).then_inc(s_rt, 1)

                def score(n):
                    dve.wait_ge(s_th, c0 + n.g + 1)
                    if h == 0:
                        dve.wait_ge(s_left, n.g + 1)
                    for t in range(GT):
                        k = n.u * GT + t
                        left = ps[5][:, t, :] if h == 0 else xr[:, k, :]
                        ch.note(V.scalar_tensor_tensor(thr[:, k, :], thr[:, k, :], 1.0, left, ALU.mult, ALU.mult,
                                                       accum_out=attr[:, n.u, t:t + 1]))
                    ch.join()
                    V.tensor_copy(att[:, n.tiles], attr[:, n.u, :]).then_inc(s_att, 1)

                def edges(n):
                    if h == 0:
                        lagged = ((norms, 0), (products, 1), (score, 2))
                    else:
                        lagged = ((products, 0), (score, 1))
                    for part, k in lagged:
                        if n.back(k).exists():
                            part(n.back(k))
                    if h > 0:
                        if n.u == 1 and n.exists():
                            dense_in(h, n)
                        if n.u == 0 and n.back(1).exists():
                            dense_out(h, n.back(1))
                groups(dve, edges, lag=2, chain=ch)

                dve.wait_ge(s_att, c0 + NG)
                if h == 0:
                    for u in range(2):
                        dve.wait_ge(s_bs[u], 32 * NI)
                else:
                    for u in range(2):
                        dve.wait_ge(s_od[u], 16 * stored(h, u))
                to_pe()
                lin4 = ps[4][0:Q, 0:2, 0:R]
                ch(V.tensor_copy(seg_x, lin4))
                whole_segments(False, seg_x)
                V.tensor_tensor(seg_x, seg_x, seg_f, ALU.subtract).then_inc(s_exp, 1)
                dve.wait_ge(s_expd, h + 1)
                whole_segments(True, seg_x)
                ch(V.reciprocal(seg_f, seg_f))
                ch.note(V.tensor_tensor(lx[0][:, :, 0:R], seg_x, seg_f, ALU.mult))
                ch.note(V.memset(lx[0][:, :, R:R + 2], 1.0))
                ch(V.memset(lx[0][:, :, R + 2:P], 0.0))
                to_pe()
                ch(V.tensor_copy(wcol[:, :], ps[0][:, :, :].rearrange("p n f -> p (n f)")[:, 0:NT]))
                ch.note(V.tensor_tensor(wfl[:, :, 0], wcol[:, :], mfl[:, 0, :], ALU.mult))
                ch(V.tensor_tensor(wfl[:, :, 1], wcol[:, :], mfl[:, 1, :], ALU.mult))

                def partial(i, u, first=False):
                    g = vec(i, u)
                    if not first:
                        dve.wait_ge(s_bp, c0 + g - 1)
                    V.tensor_copy(wflr[:, u * GT:(u + 1) * GT, :], wfl[:, bass.ds(g * GT, GT), :]).then_inc(s_wf, 1)
                partial(0, 0, True)
                partial(0, 1, True)
                with dve.Fori(1, NI) as i:
                    partial(i, 0)
                    partial(i, 1)

                dve.wait_ge(s_part, h + 1)
                part = ps[4][:, :, :].rearrange("p n f -> p (n f)")
                ch.note(V.tensor_tensor_scan(scT[:, 0, :], bcg[:, 0, :], part[:, NT:2 * NT], 0.0, ALU.mult, ALU.add))
                ch.note(V.tensor_tensor_scan(scT[:, 1, ::-1], bcg[:, 1, ::-1], part[:, 0:NT][:, ::-1], 0.0, ALU.mult, ALU.add))
                ch.note(V.memset(cT[:, 0, 0:1], 0.0))
                ch(V.memset(cT[:, 1, NT - 1:NT], 0.0))
                ch.note(V.tensor_tensor(cT[:, 0, 1:NT], bcg[:, 2, 1:NT], scT[:, 0, 0:NT - 1], ALU.mult))
                ch(V.tensor_tensor(cT[:, 1, 0:NT - 1], bcg[:, 2, 1:NT], scT[:, 1, 1:NT], ALU.mult))
                to_pe()
                V.tensor_copy(fxr.rearrange("p b k f -> p (b k) f"), ps[5][0:Q, :, :]).then_inc(s_fix, 1)

                def weights(n):
                    m = n.back(2)
                    if m.exists():
                        dve.wait_ge(s_T, c0 + m.g + 1)
                    for t in range(GT):
                        ins = V.tensor_scalar(rtT[:, n.u * GT + t, :], segbc[:, n.tile(t), :].rearrange("p a f -> p (a f)"),
                                              lcol[:, n.tile(t)], wcol[:, n.tile(t)], ALU.is_equal, ALU.mult)
                    ins.then_inc(s_w, 1)

                def aggregate(n):
                    dve.wait_ge(s_nr, c0 + n.g + 1)
                    ch(V.tensor_scalar(nrm[:, n.u, 1, :], nrm[:, n.u, 1, :], 1e-12, None, ALU.max))
                    ch(V.reciprocal(nrm[:, n.u, 2, :], nrm[:, n.u, 1, :]))
                    ch(V.tensor_tensor(nrm[:, n.u, 3, :], nrm[:, n.u, 2, :], invc[:, n.tiles], ALU.mult))
                    if h < HOPS - 1:
                        reuse(dve, s_agst[n.u], 16 * (h * NI + n.nth))
                        reuse(dve, s_sc[n.u], GT * 16 * (h * NI + n.nth))
                    V.tensor_tensor(hr[:, n.ring, :], ps[n.u][:, :, :], nrm[:, n.u, 3, :].unsqueeze(2).to_broadcast([P, GT, D]),
                                    ALU.mult).then_inc(s_ag, 1)
                    if h == HOPS - 1:
                        dve.wait_ge(s_fl[n.u], 48 * (n.nth + 1))
                        reuse(dve, s_sc[n.u], GT * 16 * (h * NI + n.nth))
                        ch.note(V.tensor_tensor(rtr[:, n.ring, :], tr[:, n.ring, :], xr[:, n.ring, :], ALU.add))
                        dve.wait_ge(s_ag, c0 + n.g + 1)
                        ch(V.tensor_tensor(hr[:, n.ring, :], hr[:, n.ring, :], relr[:, n.ring, :], ALU.add))
                        V.tensor_tensor(rtr[:, n.ring, :], rtr[:, n.ring, :], hr[:, n.ring, :], ALU.add).then_inc(s_fin, 1)

                def left_out(n):
                    dve.wait_ge(s_L, c0 + n.g + 1)
                    reuse(dve, s_Lst[n.u], 16 * (h * NI + n.nth))
                    V.tensor_copy(thr[:, n.ring, :], ps[4 + n.u][:, :, :]).then_inc(s_Le, 1)

                def sums(n):
                    for part, k in ((weights, 0), (aggregate, 1), (left_out, 2)):
                        if n.back(k).exists() and (part != left_out or h < HOPS - 1):
                            part(n.back(k))
                groups(dve, sums, lag=2, chain=ch)

        @block.scalar
        def _(act):
            A = nc.scalar

            def relu_rows(pr, u, src_, dst_, n0, n):
                for t in range(n):
                    ins = A.activation(dst_[0:pr, t, :], src_[0:pr, t, :], ACT.Relu, bias=lns[0:pr, u, LN_NB, n0 + t:n0 + t + 1],
                                       scale=lns[0:pr, u, LN_RS, n0 + t:n0 + t + 1])
                return ins

            for h in range(HOPS):
                c0 = h * NG

                def edges(n):
                    if h == 0 and n.exists():
                        act.wait_ge(s_ln, n.g + 1)
                        relu_rows(P, n.u, tr[:, n.ring4, :], tr[:, n.ring4, :], 0, GT)
                        relu_rows(P, n.u, xr[:, n.ring4, :], hr[:, n.ring, :], GT, GT).then_inc(s_lh, 1)
                        act.wait_ge(s_ohT, n.g + 1)
                        A.copy(ohT[:, :, :], ps[6][:, :, :]).then_inc(s_ohTs, 1)
                    m = n.back(1) if h == 0 else n
                    if m.exists():
                        if h == 0:
                            act.wait_ge(s_z, 16 * ND)
                        act.wait_ge(s_rtT, c0 + m.g + 1)
                        A.copy(rtT[:, m.ring, :], ps[m.u][:, :, :]).then_inc(s_rtTs, 1)
                        if h == 0:
                            act.wait_ge(s_hT, m.g + 1)
                            A.copy(hT[:, :, :], ps[4][:, :, :]).then_inc(s_hTs, 1)
                        act.wait_ge(s_rg, c0 + m.g + 1)
                        A.activation(thr[:, m.ring, :], ps[2 + m.u][:, :, :], ACT.Tanh).then_inc(s_th, 1)
                    if h > 0 and n.u == 1 and n.exists():
                        c, w, nth = chunk(h, n)
                        act.wait_ge(s_dln, c + 1)
                        relu_rows(DR, 0, xd[w], hd, 0, DC).then_inc(s_dh, 1)
                groups(act, edges, lag=1 if h == 0 else 0)
                act.wait_ge(s_exp, h + 1)
                A.activation(seg_x, seg_x, ACT.Exp).then_inc(s_expd, 1)

                def partial_out(i):
                    for u in range(2):
                        act.wait_ge(s_bp, c0 + vec(i, u) + 1)
                        reuse(act, s_bst[u], 16 * (h * NI + i))
                        A.copy(bte[:, u, :, :], ps[u][0:2, :, :]).then_inc(s_be, 1)
                partial_out(0)
                with act.Fori(1, NI) as i:
                    partial_out(i)

                spare = rtr if h < HOPS - 1 else thr

                def squares(n):
                    act.wait_ge(s_T, c0 + n.g + 1)
                    for t in range(GT):
                        A.activation(spare[:, n.u * GT + t, :], ps[n.u][:, t, :], ACT.Square, scale=invc[:, n.tile(t)],
                                     accum_out=nrm[:, n.u, 0, t:t + 1]).then_inc(s_sq, 1)
                    act.wait_ge(s_sq, GT * (c0 + n.g + 1))
                    A.activation(nrm[:, n.u, 1, :], nrm[:, n.u, 0, :], ACT.Sqrt).then_inc(s_nr, 1)

                def sums(n):
                    if n.exists():
                        squares(n)
                    m = n.back(1)
                    if h < HOPS - 1 and m.exists():
                        act.wait_ge(s_aT, c0 + m.g + 1)
                        A.copy(tr[:, m.ring, :], ps[2 + m.u][:, :, :]).then_inc(s_aTs, 1)
                groups(act, sums, lag=1)

        @block.tensor
        def _(pe):
            T = nc.tensor
            pe.wait_ge(s_const, 3)
            with pe.Fori(0, NPH) as i:
                for way, (kk, vv) in enumerate(((kbuf[0], vbuf), (kT[0], vT))):
                    pe.wait_ge(s_srt, 2 * i + way + 1)
                    for c in range(2):
                        T.transpose(ps[0][:, c, :], kk[:, c * P:(c + 1) * P], ident[:, :])
                        ins = T.transpose(ps[1][:, c, :], vv[:, c * P:(c + 1) * P], ident[:, :])
                    ins.then_inc(s_xp, 1)

            def bank(k):
                return ps[k][:, :, :].rearrange("p n f -> p (n f)")
            pe.wait_ge(s_seg, 1)
            for k in range(2):
                for b in range(2):
                    ins = T.transpose(bank(4)[0:1, k * NT + b * Q:k * NT + (b + 1) * Q], gcol[:, k, b:b + 1], ident[0:Q, 0:Q])
            ins.then_inc(s_segp, 1)

            def to_tiles(k, out_):
                for b in range(2):
                    ins = T.transpose(out_[:, b * Q:(b + 1) * Q], lx[k][:, b, :], ident[0:Q, 0:Q])
                return ins
            pe.wait_ge(s_seg, 2)
            for k in range(7):
                to_tiles(k, bank(k // 2)[:, (k % 2) * NT:(k % 2 + 1) * NT])
            T.matmul(bank(5)[:, 0:2 * NT], onesr[:, :], rows[:, WGF:WGB + 1, :].rearrange("p k n -> p (k n)"), start=True, stop=True)
            T.matmul(bank(6)[:, 0:NT], onesr[:, :], rows[:, G_, :], start=True, stop=True).then_inc(s_segp, 1)

            segs = [2]

            def asked():
                segs[0] += 1
                pe.wait_ge(s_seg, segs[0])

            def whole_segments():
                asked()
                for k, (t, r) in enumerate(((seg_f, R - 1), (seg_b, 0))):
                    for b in range(2):
                        ins = T.transpose(bank(4)[0:1, k * NT + b * Q:k * NT + (b + 1) * Q], t[:, b, r:r + 1], ident[0:Q, 0:Q])
                ins.then_inc(s_segp, 1)
                asked()
                for k in range(2):
                    for b in range(2):
                        ins = T.transpose(bank(4)[0:Q, 400 + 2 * k + b:401 + 2 * k + b], rcar[k][:, b * Q:(b + 1) * Q], ident[0:1, 0:1])
                ins.then_inc(s_segp, 1)

            def weights_to_tiles():
                asked()
                to_tiles(0, bank(0)[:, 0:NT]).then_inc(s_segp, 1)
            whole_segments()
            weights_to_tiles()

            for h in range(HOPS):
                c0 = h * NG
                def edges(n):
                    if h == 0 and n.exists():
                        pe.wait_ge(s_oh, n.g + 1)
                        for t in range(GT):
                            ins = T.transpose(ps[6][:, t, :], oh[:, t, :], ident[:, :])
                        ins.then_inc(s_ohT, 1)
                        pe.wait_ge(s_ohTs, n.g + 1)
                        reuse(pe, s_rele, n.g)
                        for t in range(GT):
                            ins = T.matmul(ps[7][:, t, :], ohT[:, t, :], emb[:, :], start=True, stop=True)
                        ins.then_inc(s_rel, 1)
                    m = n.back(1) if h == 0 else n
                    if not m.exists():
                        return
                    pe.wait_ge(s_rt, c0 + m.g + 1)
                    for t in range(GT):
                        ins = T.transpose(ps[m.u][:, t, :], rtr[:, m.u * GT + t, :], ident[:, :])
                    ins.then_inc(s_rtT, 1)
                    if h == 0:
                        pe.wait_ge(s_lh, m.g + 1)
                        for t in range(GT):
                            ins = T.transpose(ps[4][:, t, :], hr[:, m.u * GT + t, :], ident[:, :])
                        ins.then_inc(s_hT, 1)
                    pe.wait_ge(s_rtTs, c0 + m.g + 1)
                    for t in range(GT):
                        ins = T.matmul(ps[2 + m.u][:, t, :], rtT[:, m.u * GT + t, :], kw[:, :], start=True, stop=True)
                    ins.then_inc(s_rg, 1)
                    if h == 0:
                        pe.wait_ge(s_hTs, m.g + 1)
                        reuse(pe, s_att, m.g)
                        for t in range(GT):
                            ins = T.matmul(ps[5][:, t, :], hT[:, t, :], qw[:, :], start=True, stop=True)
                        ins.then_inc(s_left, 1)
                groups(pe, edges, lag=1 if h == 0 else 0)

                asked()
                for b in range(2):
                    ins = T.transpose(ps[4][0:Q, b, :], att[:, b * Q:(b + 1) * Q], ident[:, :])
                ins.then_inc(s_segp, 1)
                whole_segments()
                whole_segments()
                weights_to_tiles()

                for u in range(2):
                    pe.wait_ge(s_cp[u], 16 * NI * (h + 1))

                def partial(i, u, first=False):
                    g = vec(i, u)
                    pe.wait_ge(s_wf, c0 + g + 1)
                    if not first:
                        pe.wait_ge(s_be, c0 + g - 1)
                    for t in range(GT):
                        ins = T.matmul(ps[u][0:2, t, :], wflr[:, u * GT + t, :],
                                       rt[:, bass.ds(g * GT + t, 1), :].rearrange("p a f -> p (a f)"), start=True, stop=True)
                    ins.then_inc(s_bp, 1)
                partial(0, 0, True)
                partial(0, 1, True)
                with pe.Fori(1, NI) as i:
                    partial(i, 0)
                    partial(i, 1)
                pe.wait_ge(s_rd, 48 + 48 * h + 32)
                for k in range(2):
                    for b in range(2):
                        ins = T.transpose(bank(4)[:, k * NT + b * Q:k * NT + (b + 1) * Q], btr[:, b, k, :], ident[0:Q, 0:Q])
                ins.then_inc(s_part, 1)
                asked()
                for k in range(2):
                    for b in range(2):
                        ins = T.transpose(ps[5][0:Q, 2 * b + k, :], cT[:, k, b * Q:(b + 1) * Q], ident[:, :])
                ins.then_inc(s_segp, 1)
                pe.wait_ge(s_rd, 48 + 48 * (h + 1))

                def sums(n):
                    if n.exists():
                        pe.wait_ge(s_w, c0 + n.g + 1)
                        if n.back(2).exists():
                            pe.wait_ge(s_ag, c0 + n.g - 1)
                        for t in range(GT):
                            ins = T.matmul(ps[n.u][:, t, :], rtT[:, n.u * GT + t, :],
                                           rt[:, n.tile(t), :].rearrange("p a f -> p (a f)"), start=True, stop=True)
                        ins.then_inc(s_T, 1)
                    if h == HOPS - 1:
                        return
                    m = n.back(1)
                    if m.exists():
                        pe.wait_ge(s_ag, c0 + m.g + 1)
                        for t in range(GT):
                            ins = T.transpose(ps[2 + m.u][:, t, :], hr[:, m.u * GT + t, :], ident[:, :])
                        ins.then_inc(s_aT, 1)
                    m = n.back(2)
                    if m.exists():
                        pe.wait_ge(s_aTs, c0 + m.g + 1)
                        if m.back(2).exists():
                            pe.wait_ge(s_Le, c0 + m.g - 1)
                        for t in range(GT):
                            ins = T.matmul(ps[4 + m.u][:, t, :], tr[:, m.u * GT + t, :], qw[:, :], start=True, stop=True)
                        ins.then_inc(s_L, 1)
                groups(pe, sums, lag=2)


_INS = ['x', 'src', 'dst', 'edge_type_64', 'L0_gnn_edge_emb', 'L0_gnn_q_w', 'L0_gnn_k_w']


def kernel(**inputs):
    import numpy as _np
    import concourse.bacc as _bacc
    from concourse import mybir as _mybir
    from concourse.bass_utils import run_bass_kernel_spmd as _run

    nc = _bacc.Bacc("TRN2", target_bir_lowering=False, num_devices=1)
    arrays, args = {}, []
    for name in _INS:
        a = _np.ascontiguousarray(inputs[name])
        arrays[f"in_{name}_dram"] = a
        args.append(nc.dram_tensor(f"in_{name}_dram", a.shape, _mybir.dt.from_np(a.dtype), kind="ExternalInput").ap())
    args.append(nc.dram_tensor("out_0_dram", (50000, 128), _mybir.dt.float32, kind="ExternalOutput").ap())
    gnn_kernel(nc, *args)
    r = _run(nc, [arrays], core_ids=[0])
    return r.results[0]["out_0_dram"]
```

```python
from contextlib import ExitStack

import concourse.bass as bass
from concourse import mybir

F32 = mybir.dt.float32
I32 = mybir.dt.int32
U8 = mybir.dt.uint8
ALU = mybir.AluOpType
ACT = mybir.ActivationFunctionType

N, E, D, NREL = 50000, 25000, 128, 64
HOPS = 3
R = 125
NT = E // R
P = 128
NS = NT * P
Q = NT // 2
GT = 4
NG = NT // GT
NI = NG // 2
TS = 4
NF = NG // TS
SC = 256
LOGN = 15
DR = 125
DK = N // DR
DC = 8
ND = DK // DC
BIG = 3.0e38
EPS = 1e-5
PADKEY = 65536.0
NOSEG = 200.0
NTYPES_PAD = 64.0
LN_SUM, LN_DIF, LN_Q, LN_D2, LN_V, LN_VE, LN_Y, LN_A, LN_RS, LN_NB = range(10)
RSQRT_BITS = 1597463007.0
NPH = LOGN - 8


def gnn_kernel(nc, x, src, dst, etype, edge_emb, q_w, k_w, out):
    ctx = ExitStack()
    with ctx:
        def sb(name, shape, dt=F32):
            return ctx.enter_context(nc.sbuf_tensor(name, shape, dt))

        def sem(name):
            return ctx.enter_context(nc.semaphore(name))

        def dram(name, shape, dt=F32):
            return nc.dram_tensor(name, shape, dt, kind="Internal").ap()

        hs_d = dram("hs_d", [32768 + 128])
        vs_d = dram("vs_d", [32768])
        lid_d = dram("lid_d", [NS], U8)
        ntab_d = dram("ntab_d", [N, D])
        rel_d = dram("rel_d", [NS, D])
        acc_d = [dram(f"acc{k}_d", [NS, D]) for k in range(HOPS)]
        left_d = [dram(f"left{k}_d", [NS, D]) for k in range(2)]
        bt_d = dram("bt_d", [2, NT * D])
        fx_d = dram("fx_d", [2, NT * D])

        def slots(t):
            return t[0:NS, :].rearrange("(n p) f -> p n f", p=P)

        rt = sb("rt", [P, NT, D])
        segbc = sb("segbc", [P, NT, P], U8)
        tr = sb("tr", [P, TS * GT, D])
        xr = sb("xr", [P, TS * GT, D])
        relr = sb("relr", [P, 2 * GT, D])
        rtr = sb("rtr", [P, 2 * GT, D])
        rtT = sb("rtT", [P, 2 * GT, D])
        thr = sb("thr", [P, 2 * GT, D])
        hr = sb("hr", [P, 2 * GT, D])
        hT = sb("hT", [P, GT, D])
        minus1 = sb("minus1", [1, 1])
        ident = sb("ident", [P, P])
        kw = sb("kw", [D, D])
        qw = sb("qw", [D, D])
        emb = sb("emb", [P, D])
        iota_c = sb("iota_c", [P, P])
        ohT = sb("ohT", [P, GT, P])
        oh = sb("oh", [P, GT, P])
        onesr = sb("onesr", [1, P])
        stats = sb("stats", [P, 2 * GT, 6])
        lns = sb("lns", [P, 2, 10, 2 * GT])
        flat = rt[:, :, :].rearrange("p n f -> p (n f)")
        kbuf = [flat[:, i * SC:(i + 1) * SC] for i in range(2)]
        kT = [flat[:, (2 + i) * SC:(3 + i) * SC] for i in range(2)]
        vbuf = flat[:, 4 * SC:5 * SC]
        vT = flat[:, 5 * SC:6 * SC]
        swapm = flat[:, 6 * SC:6 * SC + 128]
        swapd = flat[:, 7 * SC:7 * SC + 128]
        raws = [flat[:, (8 + i) * SC:(9 + i) * SC].bitcast(I32) for i in range(3)]
        sgn = [flat[:, (11 + i) * SC:(12 + i) * SC] for i in range(8)]
        xd = [xr[0:DR, 2 * GT:4 * GT, :], hr[0:DR, :, :]]
        hd = sb("hd", [DR, DC, D])
        pbits = sb("pbits", [P, 9], I32)
        sgnp = sb("sgnp", [P, 9])
        hp = sb("hp", [Q, 2, R + 2])
        vl = sb("vl", [Q, 2, R])
        vi = sb("vi", [Q, 2, R], I32)
        ti = sb("ti", [Q, 2, R], I32)
        gf = sb("gf", [Q, 2, R])
        gb = sb("gb", [Q, 2, R])
        gfn = sb("gfn", [Q, 2, R])
        gbn = sb("gbn", [Q, 2, R])
        def lin(ring, k, w):
            return ring[0:Q, 0:2 * GT, :].rearrange("p n f -> p (n f)")[:, k * 2 * P:k * 2 * P + 2 * w].rearrange("p (b r) -> p b r", b=2)
        seg_x, seg_xf, seg_xb, seg_f = (lin(tr, k, R) for k in range(4))
        seg_b = lin(xr, 0, R)
        lx = [lin(xr, k, P) for k in range(1, 4)] + [lin(relr, k, P) for k in range(4)]
        LH, LT, LS, LY, LL, LF, LB = range(7)
        lid8 = sb("lid8", [Q, 2, P], U8)
        gcol = sb("gcol", [Q, 2, 2])
        rows = sb("rows", [1, 8, NT])
        G_, GN, WGF, WGB, GNEG, GNNEG, WGFN, WGBN = range(8)
        thrf = thr[0:1, :, :].rearrange("p n f -> p (n f)")
        hrf = hr[0:1, :, :].rearrange("p n f -> p (n f)")
        whrow = thrf[:, 0:NT]
        rscan = [thrf[:, (1 + k) * NT:(2 + k) * NT] for k in range(2)]
        rcar = [hrf[:, k * NT:(k + 1) * NT] for k in range(2)]
        lcol = sb("lcol", [P, NT])
        hidx = sb("hidx", [P, NT], I32)
        tidx = sb("tidx", [P, NT], I32)
        lidx = sb("lidx", [P, NT], I32)
        tycol = sb("tycol", [P, NT])
        mfl = sb("mfl", [P, 2, NT])
        invc = sb("invc", [P, NT])
        att = sb("att", [P, NT])
        wcol = sb("wcol", [P, NT])
        wfl = sb("wfl", [P, NT, 2])
        wflr = sb("wflr", [P, 2 * GT, 2])
        bcg = sb("bcg", [P, 3, NT])
        scT = relr[:, :, :].rearrange("p n f -> p (n f)")[:, 0:2 * NT].rearrange("p (k n) -> p k n", k=2)
        cT = tr[:, :, :].rearrange("p n f -> p (n f)")[:, 0:2 * NT].rearrange("p (k n) -> p k n", k=2)
        attr = sb("attr", [P, 2, GT])
        nrm = sb("nrm", [P, 2, 4, GT])
        stg = sb("stg", [P, TS, GT], I32)
        stg2 = sb("stg2", [P, TS, GT], I32)
        btr = hr[0:Q, 0:4, :].rearrange("p (b k) f -> p b k f", b=2)
        fxr = hr[0:Q, 4:8, :].rearrange("p (b k) f -> p b k f", b=2)
        bte = thr[0:2, :, :].rearrange("a (u t) f -> a u t f", u=2)

        ps = [ctx.enter_context(nc.psum_tensor(f"ps{i}", [P, GT, D], F32)) for i in range(8)]

        s_ld = sem("s_ld")
        s_const = sem("s_const")
        s_dve = sem("s_dve")
        s_srt = sem("s_srt")
        s_part = sem("s_part")
        s_sq = sem("s_sq")
        s_xp = sem("s_xp")
        s_seg = sem("s_seg")
        s_segp = sem("s_segp")
        s_exp = sem("s_exp")
        s_expd = sem("s_expd")
        s_wr = sem("s_wr")
        s_rd = sem("s_rd")
        s_go = sem("s_go")
        s_z = sem("s_z")
        s_xd = [sem(f"s_xd{u}") for u in range(2)]
        s_od = [sem(f"s_od{u}") for u in range(2)]
        s_dln = sem("s_dln")
        s_dh = sem("s_dh")
        s_do = sem("s_do")
        s_t = [sem(f"s_t{u}") for u in range(TS)]
        s_rl = [sem(f"s_rl{u}") for u in range(2)]
        s_lf = [sem(f"s_lf{u}") for u in range(2)]
        s_cp = [sem(f"s_cp{u}") for u in range(2)]
        s_bs = [sem(f"s_bs{u}") for u in range(2)]
        s_rt = sem("s_rt")
        s_att = sem("s_att")
        s_rtT = sem("s_rtT")
        s_rtTs = sem("s_rtTs")
        s_rg = sem("s_rg")
        s_th = sem("s_th")
        s_ln = sem("s_ln")
        s_lh = sem("s_lh")
        s_oh = sem("s_oh")
        s_ohT = sem("s_ohT")
        s_ohTs = sem("s_ohTs")
        s_rel = sem("s_rel")
        s_rele = sem("s_rele")
        s_base = sem("s_base")
        s_hT = sem("s_hT")
        s_hTs = sem("s_hTs")
        s_left = sem("s_left")
        s_wf = sem("s_wf")
        s_bp = sem("s_bp")
        s_be = sem("s_be")
        s_bst = [sem(f"s_bst{u}") for u in range(2)]
        s_w = sem("s_w")
        s_T = sem("s_T")
        s_nr = sem("s_nr")
        s_ag = sem("s_ag")
        s_aT = sem("s_aT")
        s_aTs = sem("s_aTs")
        s_L = sem("s_L")
        s_Le = sem("s_Le")
        s_Lst = [sem(f"s_Lst{u}") for u in range(2)]
        s_al = [sem(f"s_al{r}") for r in range(TS)]
        s_as = [sem(f"s_as{r}") for r in range(TS)]
        s_acc = sem("s_acc")
        s_sc = [sem(f"s_sc{r}") for r in range(TS)]
        s_zero = sem("s_zero")
        s_hop = sem("s_hop")
        s_pace = sem("s_pace")
        s_pool = sem("s_pool")
        s_fix = sem("s_fix")

        PADROWS = (E // SC, E % SC)
        LOADS = 0
        def runs(t):
            return t.rearrange("(p n) f -> p n f", p=DR)
        block = ctx.enter_context(nc.Block())

        class Group:

            def __init__(self, i, r):
                self.i, self.slot = (i + r // TS if r // TS else i), r % TS
                self.g = self.i * TS + self.slot
                self.u = self.slot % 2
                self.nth = self.i * 2 + self.slot // 2
                self.tiles = bass.ds(self.g * GT, GT)
                self.ring = slice(self.u * GT, (self.u + 1) * GT)
                self.ring4 = slice(self.slot * GT, (self.slot + 1) * GT)

            def back(self, k):
                return Group(self.i, self.slot - k)

            def tile(self, t):
                return bass.ds(self.g * GT + t, 1)

            def exists(self, k=0):
                return not isinstance(self.g, int) or 0 <= self.g + k < NG

        def groups(eng, step, lag=0, chain=None):
            for i in range(2):
                if chain is not None:
                    before = chain.at
                for r in range(TS):
                    step(Group(i, r))
            if chain is not None:
                start, per = before, chain.at - before
            with eng.Fori(2, NF) as i:
                if chain is not None:
                    chain.at = start + (i - 1) * per
                for r in range(TS):
                    step(Group(i, r))
            if chain is not None:
                chain.at = start + (NF - 1) * per
            for r in range(NG % TS + lag):
                step(Group(NF, r))

        of_slot = [NF + (r < NG % TS) for r in range(TS)]

        def turn(h, n):
            return h * of_slot[n.slot] + n.i + 1

        def chunk(h, n):
            k = (h - 1) * NI + n.slot // 2
            return k + n.i * 2, k % 2, k // 2 + n.i

        def stored(h, w):
            return (h * NI + 1 - w) // 2

        def vec(i, u):
            return 2 * i + u

        def reuse(eng, sem_, value):
            if not isinstance(value, int) or value > 0:
                eng.wait_ge(sem_, value)

        N_BIDIR = 2
        SETUP_SEG = 2 + N_BIDIR + 1 + 1

        @block.sync
        def _(sp):
            whole, rest = PADROWS
            sp.wait_ge(s_zero, 1)
            for t, a in zip(raws, (src, dst, etype)):
                sp.dma_start(t[0:whole, :], a[0:whole * SC].rearrange("(p c) -> p c", c=SC)).then_inc(s_ld, 16)
                sp.dma_start(t[whole:whole + 1, 0:rest], a[whole * SC:E].rearrange("(p c) -> p c", p=1)).then_inc(s_ld, 16)
            sp.dma_start(kw[:, :], k_w[:, :]).then_inc(s_ld, 16)
            sp.dma_start(qw[:, :], q_w[:, :]).then_inc(s_ld, 16)
            sp.dma_start(emb[0:NREL, :], edge_emb[:, :]).then_inc(s_ld, 16)
            with sp.Fori(0, ND) as i:
                sp.dma_start(runs(ntab_d)[:, bass.ds(i * DC, DC), :], rtT[0:DR, :, :]).then_inc(s_z, 16)

            sp.wait_ge(s_go, 1)
            sp.dma_start(hs_d[0:1].rearrange("(a b) -> a b", a=1), minus1[:, :]).then_inc(s_wr, 16)
            sp.dma_start(hs_d[1:32769].rearrange("(p c) -> p c", c=SC), kbuf[0]).then_inc(s_wr, 16)
            sp.dma_start(vs_d.rearrange("(p c) -> p c", c=SC), vbuf).then_inc(s_wr, 16)
            sp.wait_ge(s_wr, 48)
            hs_v = bass.AP(tensor=hs_d.tensor, offset=0, ap=[[R, Q], [R * Q, 2], [1, R + 2]])
            sp.dma_start(hp[:, :, :], hs_v).then_inc(s_rd, 16)
            sp.dma_start(vl[:, :, :], vs_d[0:E].rearrange("(b q r) -> q b r", b=2, r=R)).then_inc(s_rd, 16)
            sp.wait_ge(s_go, 2)
            sp.dma_start(lid_d.rearrange("(b q r) -> q b r", b=2, r=P), lid8[:, :, :]).then_inc(s_wr, 16)
            sp.wait_ge(s_wr, 64)
            sp.dma_start(segbc[:, :, :].rearrange("p n f -> p (n f)"),
                         lid_d[:].rearrange("(a b) -> a b", a=1).broadcast_to([P, NS])).then_inc(s_rd, 16)

            wr, rd = 64, 48
            for h in range(HOPS):
                c0 = h * NG
                def load_rel(n):
                    sp.dma_start(relr[:, n.ring, :], slots(rel_d)[:, n.tiles, :]).then_inc(s_rl[n.u], 16)

                def load_left(n):
                    sp.dma_start(xr[:, n.ring, :], slots(left_d[h - 1])[:, n.tiles, :]).then_inc(s_lf[n.u], 16)

                def load_x(n):
                    c, w, nth = chunk(h, n)
                    sp.dma_start(xd[w], runs(x)[:, bass.ds(c * DC, DC), :]).then_inc(s_xd[w], 16)

                def edges(n):
                    if n.exists():
                        sp.wait_ge(s_rt, c0 + n.g + 1)
                        sp.dma_start(rt[:, n.tiles, :], rtr[:, n.ring, :]).then_inc(s_cp[n.u], 16)
                        if h == 0:
                            sp.dma_start(slots(rel_d)[:, n.tiles, :], relr[:, n.ring, :]).then_inc(s_bs[n.u], 16)
                            sp.dma_start(slots(acc_d[0])[:, n.tiles, :], xr[:, n.ring4, :]).then_inc(s_bs[n.u], 16)
                            return
                        if n.exists(2):
                            load_rel(n.back(-2))
                        if n.back(2).exists():
                            sp.wait_ge(s_att, c0 + n.g - 1)
                            load_left(n)
                    if n.u == 0 and n.back(1).exists():
                        c, w, nth = chunk(h, n.back(1))
                        sp.wait_ge(s_do, c + 1)
                        sp.dma_start(runs(out)[:, bass.ds(c * DC, DC), :], xd[w]).then_inc(s_od[w], 16)
                    if n.u == 1 and n.back(2).exists() and n.exists(2):
                        c, w, nth = chunk(h, n.back(2))
                        sp.wait_ge(s_od[w], 16 * (nth + 1))
                        load_x(n.back(-2))
                if h > 0:
                    for k in range(2):
                        load_rel(Group(0, k))
                        load_left(Group(0, k))
                    for w in range(2):
                        reuse(sp, s_od[w], 16 * stored(h - 1, w))
                    load_x(Group(0, 1))
                    load_x(Group(0, 3))
                groups(sp, edges, lag=1 if h > 0 else 0)
                if h == 0:
                    for u in range(2):
                        sp.wait_ge(s_bs[u], 32 * NI)
                with sp.Fori(0, NI) as i:
                    for u in range(2):
                        g = vec(i, u)
                        sp.wait_ge(s_be, c0 + g + 1)
                        sp.dma_start(bt_d[:, bass.ds(g * GT * D, GT * D)], bte[:, u, :, :].rearrange("a t f -> a (t f)")).then_inc(s_bst[u], 16)
                for u in range(2):
                    sp.wait_ge(s_bst[u], 16 * NI * (h + 1))
                for k in range(2):
                    sp.dma_start(btr[:, :, k, :], bt_d[k, :].rearrange("(b q f) -> q b f", b=2, f=D)).then_inc(s_rd, 16)
                rd += 32
                sp.wait_ge(s_fix, h + 1)
                for k in range(2):
                    sp.dma_start(fx_d[k, :].rearrange("(b q f) -> q b f", b=2, f=D), fxr[:, :, k, :]).then_inc(s_wr, 16)
                wr += 32
                sp.wait_ge(s_wr, wr)
                sp.dma_start(rt[R:R + 2, :, :].rearrange("a n f -> a (n f)"), fx_d[:, :]).then_inc(s_rd, 16)
                rd += 16

                def results(n):
                    if n.exists():
                        m = n.back(TS)
                        if m.exists():
                            if h < HOPS - 1:
                                sp.wait_ge(s_as[m.slot], 16 * turn(h, m))
                            else:
                                sp.wait_ge(s_sc[m.slot], GT * 16 * turn(h, m))
                        sp.dma_start(xr[:, n.ring4, :], slots(acc_d[h])[:, n.tiles, :]).then_inc(s_al[n.slot], 16)
                    if h == HOPS - 1:
                        return
                    m = n.back(2)
                    if m.exists():
                        sp.wait_ge(s_acc, c0 + m.g + 1)
                        sp.dma_start(slots(acc_d[h + 1])[:, m.tiles, :], xr[:, m.ring4, :]).then_inc(s_as[m.slot], 16)
                    m = n.back(3)
                    if m.exists():
                        sp.wait_ge(s_Le, c0 + m.g + 1)
                        sp.dma_start(slots(left_d[h])[:, m.tiles, :], thr[:, m.ring, :]).then_inc(s_Lst[m.u], 16)
                groups(sp, results, lag=3)
                if h < HOPS - 1:
                    for r in range(TS):
                        sp.wait_ge(s_as[r], 16 * of_slot[r] * (h + 1))
                    for u in range(2):
                        sp.wait_ge(s_Lst[u], 16 * NI * (h + 1))
            for r in range(TS):
                sp.wait_ge(s_sc[r], HOPS * 16 * GT * of_slot[r])
            for u in range(2):
                sp.wait_ge(s_od[u], 16 * (ND // 2))
                sp.wait_ge(s_bs[u], 32 * NI)

        @block.gpsimd
        def _(pool):
            def pool_wait(sem_, value):
                pool.wait_ge(sem_, value)
                pool.sem_inc(s_pace, 1)

            def reuse_pool(sem_, value):
                if not isinstance(value, int) or value > 0:
                    pool_wait(sem_, value)
            nc.gpsimd.iota(iota_c[:, :], pattern=[[1, P]], base=0, channel_multiplier=0,
                           allow_small_or_imprecise_dtypes=True).then_inc(s_const, 1)
            nc.gpsimd.memset(ident[:, :], 1.0).then_inc(s_const, 1)
            pool.wait_ge(s_const, 2)
            nc.gpsimd.affine_select(ident[:, :], ident[:, :], pattern=[[1, P]], base=0, channel_multiplier=-1,
                                    compare_op=ALU.is_equal, fill=0.0).then_inc(s_const, 1)
            for k in range(1, 8):
                nc.gpsimd.iota(sgn[k], pattern=[[0, SC >> (k + 1)], [-2, 2], [0, 1 << k]], base=1, channel_multiplier=0,
                               allow_small_or_imprecise_dtypes=True).then_inc(s_const, 1)
            nc.gpsimd.iota(pbits[:, 8:9], pattern=[[0, 1]], base=0, channel_multiplier=1).then_inc(s_const, 1)

            pool.wait_ge(s_go, 4)

            staged = [0, 0]

            def staging(n, k):
                return staged[0] + n.g * staged[1] + k

            def scatter(n, table, rows):
                for t in range(GT):
                    nc.gpsimd.indirect_dma_start(out=table[:, :], out_offset=bass.IndirectOffsetOnAxis(ap=stg[:, n.slot, t:t + 1], axis=0),
                                                 in_=rows[:, n.slot * GT + t, :], in_offset=None, bounds_check=N - 1,
                                                 oob_is_err=False).then_inc(s_sc[n.slot], 16)

            for h in range(HOPS):
                c0 = h * NG

                def fetch(n):
                    if h == 0:
                        m = n.back(TS)
                        if m.exists():
                            pool_wait(s_rt, m.g + 1)
                            pool_wait(s_bs[m.u], 32 * (m.nth + 1))
                    else:
                        pool_wait(s_rt, c0 - TS + n.g + 1)
                    nc.gpsimd.tensor_copy(stg[:, n.slot, :], tidx[:, n.tiles]).then_inc(s_pool, 1)
                    if h == 0:
                        nc.gpsimd.tensor_copy(stg2[:, n.slot, :], hidx[:, n.tiles]).then_inc(s_pool, 1)
                    pool_wait(s_pool, staging(n, staged[1]))
                    for t in range(GT):
                        k = n.slot * GT + t
                        nc.gpsimd.indirect_dma_start(out=tr[:, k, :], out_offset=None, in_=(x if h == 0 else ntab_d)[:, :],
                                                     in_offset=bass.IndirectOffsetOnAxis(ap=stg[:, n.slot, t:t + 1], axis=0)).then_inc(s_t[n.slot], 16)
                        if h == 0:
                            nc.gpsimd.indirect_dma_start(out=xr[:, k, :], out_offset=None, in_=x[:, :],
                                                         in_offset=bass.IndirectOffsetOnAxis(ap=stg2[:, n.slot, t:t + 1], axis=0)).then_inc(s_t[n.slot], 16)
                if h > 0:
                    for r in range(TS):
                        pool.wait_ge(s_sc[r], 16 * GT * of_slot[r] * h)
                    pool.wait_ge(s_acc, NG * h)
                    pool.wait_ge(s_aTs, NG * h)
                staged[1] = 2 if h == 0 else 1
                groups(pool, fetch)
                staged[0] += NG * staged[1]

                if h == 0:
                    pool.wait_ge(s_z, 16 * ND)
                pool.wait_ge(s_rt, c0 + NG)
                if h == HOPS - 1:
                    for u in range(2):
                        pool.wait_ge(s_od[u], 16 * (ND // 2))
                staged[1] = 1

                def put(n):
                    m = n.back(TS)
                    if m.exists():
                        pool_wait(s_sc[m.slot], 16 * GT * turn(h, m))
                    nc.gpsimd.tensor_copy(stg[:, n.slot, :], lidx[:, n.tiles]).then_inc(s_pool, 1)
                    pool_wait(s_pool, staging(n, 1))
                    if h < HOPS - 1:
                        pool_wait(s_ag, c0 + n.g + 1)
                        scatter(n, ntab_d, tr)
                    else:
                        pool_wait(s_acc, c0 + n.g + 1)
                        scatter(n, out, xr)
                groups(pool, put)
                staged[0] += NG

        @block.vector
        def _(dve):
            V = nc.vector

            class Chain:
                at = 0

                def note(self, ins):
                    self.at = self.at + 1
                    ins.then_inc(s_dve, 1)

                def join(self):
                    dve.wait_ge(s_dve, self.at)

                def __call__(self, ins):
                    self.note(ins)
                    self.join()
            ch = Chain()

            ch.note(V.memset(minus1[:, :], -1.0))
            ch.note(V.memset(onesr[:, :], 1.0))
            ch.note(V.memset(raws[0], int(PADKEY)))
            ch.note(V.memset(raws[1], 0))
            ch.note(V.memset(raws[2], 0))
            ch.note(V.memset(emb[:, :], 0.0))
            ch(V.memset(rtT[:, :, :], 0.0))
            dve.sem_inc(s_zero, 1)

            def layer_norm(pr, u, n, s_out, between=()):
                between = list(between)

                def step(ins):
                    ch.note(ins)
                    done = ch.at
                    if between:
                        between.pop(0)()
                    dve.wait_ge(s_dve, done)

                def L(k):
                    return lns[0:pr, u, k, 0:n]
                me, qe, mo, qo = (stats[0:pr, 0:n, k] for k in (1, 2, 4, 5))
                ch.note(V.tensor_tensor(L(LN_SUM), me, mo, ALU.add))
                ch.note(V.tensor_tensor(L(LN_DIF), me, mo, ALU.subtract))
                step(V.tensor_tensor(L(LN_Q), qe, qo, ALU.add))
                step(V.tensor_tensor(L(LN_D2), L(LN_DIF), L(LN_DIF), ALU.mult))
                step(V.scalar_tensor_tensor(L(LN_V), L(LN_D2), D / 4.0, L(LN_Q), ALU.mult, ALU.add))
                step(V.tensor_scalar(L(LN_VE), L(LN_V), 1.0 / D, EPS, ALU.mult, ALU.add))
                step(V.tensor_scalar(L(LN_Y).bitcast(I32), L(LN_VE).bitcast(I32), -0.5, RSQRT_BITS, ALU.mult, ALU.add))
                y = LN_Y
                for k in range(3):
                    to = LN_RS if y == LN_Y else LN_Y
                    step(V.scalar_tensor_tensor(L(LN_A), L(y), -0.5, L(y), ALU.mult, ALU.mult))
                    step(V.tensor_tensor(L(LN_A), L(LN_A), L(LN_VE), ALU.mult))
                    step(V.scalar_tensor_tensor(L(to), L(LN_A), 1.5, L(y), ALU.add, ALU.mult))
                    y = to
                V.scalar_tensor_tensor(L(LN_NB), L(LN_SUM), -0.5, L(LN_RS), ALU.mult, ALU.mult).then_inc(s_out, 1)
                assert not between

            def dense_in(h, n, between):
                c, w, nth = chunk(h, n)
                dve.wait_ge(s_xd[w], 16 * (nth + 1))
                for t in range(DC):
                    ch.note(V.bn_stats(stats[0:DR, t, :], xd[w][:, t, :]))
                ch.join()
                layer_norm(DR, 0, DC, s_dln, between)

            def dense_out(h, n):
                c, w, nth = chunk(h, n)
                dve.wait_ge(s_dh, c + 1)
                V.scalar_tensor_tensor(xd[w].rearrange("p n f -> p (n f)"), hd[:, :, :].rearrange("p n f -> p (n f)"), 3.0,
                                       xd[w].rearrange("p n f -> p (n f)"), ALU.mult, ALU.add).then_inc(s_do, 1)

            dve.wait_ge(s_ld, 16 * 9)
            ch.note(V.tensor_copy(kbuf[0], raws[0]))
            ch.note(V.scalar_tensor_tensor(vbuf, raws[1], float(NREL), raws[2], ALU.mult, ALU.add))
            dve.wait_ge(s_const, 11)
            for k in range(8):
                ch.note(V.tensor_scalar(pbits[:, k:k + 1], pbits[:, 8:9], k, 1, ALU.logical_shift_right, ALU.bitwise_and))
            ch.join()
            ch(V.tensor_scalar(sgnp[:, 0:8], pbits[:, 0:8], -2.0, 1.0, ALU.mult, ALU.add))

            def exchange(a_buf, b_buf, v, stride):
                def halves(t):
                    w = t.rearrange("p (n t s) -> p n t s", t=2, s=stride)
                    return w[:, :, 0, :], w[:, :, 1, :]
                ka, kb = halves(a_buf)
                na, nb = halves(b_buf)
                va, vb = halves(v)
                m = swapm.rearrange("p (n s) -> p n s", s=stride)
                d = swapd.rearrange("p (n s) -> p n s", s=stride)
                ch.note(V.tensor_tensor(m, ka, kb, ALU.is_gt))
                ch.note(V.tensor_tensor(d, vb, va, ALU.subtract))
                ch.note(V.tensor_tensor(na, ka, kb, ALU.min))
                dve.wait_ge(s_dve, ch.at - 1)
                ch.note(V.tensor_tensor(d, d, m, ALU.mult))
                ch.note(V.tensor_tensor(nb, ka, kb, ALU.max))
                dve.wait_ge(s_dve, ch.at - 1)
                ch.note(V.tensor_tensor(va, va, d, ALU.add))
                ch(V.tensor_tensor(vb, vb, d, ALU.subtract))

            def apply_sign(t, k):
                if 1 <= k < 8:
                    ch(V.tensor_tensor(t, t, sgn[k], ALU.mult))
                elif 8 <= k < LOGN:
                    ch(V.tensor_scalar(t, t, sgnp[:, k - 8:k - 7], None, ALU.mult))

            at, hand = 0, 0
            for k in range(1, LOGN + 1):
                apply_sign(kbuf[at], k - 1)
                apply_sign(kbuf[at], k)
                if k > 8:
                    dve.sem_inc(s_srt, 1)
                    hand += 1
                    dve.wait_ge(s_xp, hand)
                    bt = (k - 8) % 2
                    ch.note(V.tensor_copy(kT[bt], ps[0][:, 0:2, :].rearrange("p n f -> p (n f)")))
                    ch(V.tensor_copy(vT, ps[1][:, 0:2, :].rearrange("p n f -> p (n f)")))
                    for m in range(k - 1, 7, -1):
                        exchange(kT[bt], kT[1 - bt], vT, 1 << (m - 8))
                        bt = 1 - bt
                    dve.sem_inc(s_srt, 1)
                    hand += 1
                    dve.wait_ge(s_xp, hand)
                    ch.note(V.tensor_copy(kbuf[0], ps[0][:, 0:2, :].rearrange("p n f -> p (n f)")))
                    ch(V.tensor_copy(vbuf, ps[1][:, 0:2, :].rearrange("p n f -> p (n f)")))
                for m in range(min(k, 8) - 1, -1, -1):
                    exchange(kbuf[at], kbuf[1 - at], vbuf, 1 << m)
                    at = 1 - at
            assert at == 0
            dve.sem_inc(s_go, 1)

            dve.wait_ge(s_rd, 32)
            cur, first, last_ = hp[:, :, 1:R + 1], hp[:, :, 1:2], hp[:, :, R:R + 1]
            ch.note(V.tensor_tensor(gf[:, :, :], hp[:, :, 0:R], cur, ALU.is_equal))
            ch.note(V.tensor_tensor(gb[:, :, :], hp[:, :, 2:R + 2], cur, ALU.is_equal))
            ch(V.tensor_copy(vi[:, :, :], vl[:, :, :]))
            ch.note(V.tensor_copy(gcol[:, 0, :], gf[:, :, 0:1].rearrange("p b o -> p (b o)")))
            V.tensor_tensor(gcol[:, 1, :], first.rearrange("p b o -> p (b o)"), last_.rearrange("p b o -> p (b o)"),
                            ALU.is_equal).then_inc(s_seg, 1)
            ch.note(V.scalar_tensor_tensor(lx[LL][:, :, 0:R], gb[:, :, :], PADKEY, cur, ALU.mult, ALU.add))
            ch.note(V.memset(lx[LL][:, :, R:P], PADKEY))
            ch.note(V.tensor_copy(lx[LH][:, :, 0:R], cur))
            ch.note(V.memset(lx[LH][:, :, R:P], 0.0))
            ch.note(V.memset(lx[LT][:, :, R:P], 0.0))
            ch.note(V.memset(lx[LY][:, :, R:P], NTYPES_PAD))
            ch.note(V.tensor_tensor(lx[LF][:, :, 0:R], cur, first.to_broadcast([Q, 2, R]), ALU.is_equal))
            ch.note(V.tensor_tensor(lx[LB][:, :, 0:R], cur, last_.to_broadcast([Q, 2, R]), ALU.is_equal))
            ch.note(V.memset(lx[LF][:, :, R:P], 0.0))
            ch.note(V.memset(lx[LB][:, :, R:P], 0.0))
            ch.note(V.tensor_scalar(ti[:, :, :], vi[:, :, :], 6, None, ALU.logical_shift_right))
            ch(V.tensor_scalar(vi[:, :, :], vi[:, :, :], NREL - 1, None, ALU.bitwise_and))
            ch.note(V.tensor_copy(lx[LT][:, :, 0:R], ti[:, :, :]))
            ch.note(V.tensor_copy(lx[LY][:, :, 0:R], vi[:, :, :]))
            ch.note(V.tensor_scalar(seg_x, gf[:, :, :], -1.0, 1.0, ALU.mult, ALU.add))
            ch(V.memset(seg_xf, 1.0))
            ch.note(V.memset(seg_x[:, :, 0:1], 0.0))
            ch.note(V.memset(seg_xf[:, :, 0:1], 0.0))
            ch.note(V.memset(gf[:, :, 0:1], 0.0))
            ch(V.memset(gb[:, :, R - 1:R], 0.0))
            flat2 = "p b r -> p (b r)"
            ch(V.tensor_tensor_scan(seg_f.rearrange(flat2), seg_xf.rearrange(flat2), seg_x.rearrange(flat2), 0.0, ALU.mult, ALU.add))
            ch.note(V.tensor_copy(lx[LS][:, :, 0:R], seg_f))
            ch.note(V.memset(lx[LS][:, :, R:R + 1], 0.0))
            ch.note(V.tensor_copy(lx[LS][:, :, R + 1:R + 2], seg_f[:, :, R - 1:R]))
            ch.note(V.memset(lx[LS][:, :, R + 2:P], NOSEG))
            ch.note(V.tensor_scalar(gfn[:, :, :], gf[:, :, :], BIG, -BIG, ALU.mult, ALU.add))
            ch(V.tensor_scalar(gbn[:, :, :], gb[:, :, :], BIG, -BIG, ALU.mult, ALU.add))
            V.tensor_copy(lid8[:, :, :], lx[LS]).then_inc(s_go, 1)
            dve.wait_ge(s_segp, 1)
            row = ps[4][0:1, :, :].rearrange("p n f -> p (n f)")
            ch.note(V.tensor_copy(rows[:, G_, :], row[:, 0:NT]))
            ch(V.tensor_copy(whrow, row[:, NT:2 * NT]))
            ch.note(V.tensor_copy(rows[:, GN, 0:NT - 1], rows[:, G_, 1:NT]))
            ch(V.memset(rows[:, GN, NT - 1:NT], 0.0))
            ch.note(V.tensor_tensor(rows[:, WGF, :], rows[:, G_, :], whrow, ALU.mult))
            ch(V.tensor_tensor(rows[:, WGB, :], rows[:, GN, :], whrow, ALU.mult))
            for a, b in ((G_, GNEG), (GN, GNNEG), (WGF, WGFN), (WGB, WGBN)):
                ch.note(V.tensor_scalar(rows[:, b, :], rows[:, a, :], BIG, -BIG, ALU.mult, ALU.add))
            ch.join()
            dve.sem_inc(s_seg, 1)
            dve.wait_ge(s_segp, 2)

            def tile_of(k):
                return ps[k // 2][:, :, :].rearrange("p n f -> p (n f)")[:, (k % 2) * NT:(k % 2 + 1) * NT]
            ch.note(V.tensor_copy(hidx[:, :], tile_of(LH)))
            ch.note(V.tensor_copy(tidx[:, :], tile_of(LT)))
            ch.note(V.tensor_copy(lcol[:, :], tile_of(LS)))
            ch.note(V.tensor_copy(tycol[:, :], tile_of(LY)))
            ch.note(V.tensor_copy(lidx[:, :], tile_of(LL)))
            ch.note(V.tensor_copy(mfl[:, 0, :], tile_of(LF)))
            ch.note(V.tensor_copy(mfl[:, 1, :], tile_of(LB)))
            ch.note(V.tensor_copy(bcg[:, 0:2, :], ps[5][:, :, :].rearrange("p n f -> p (n f)")[:, 0:2 * NT].rearrange("p (k n) -> p k n", k=2)))
            ch(V.tensor_copy(bcg[:, 2, :], ps[6][:, :, :].rearrange("p n f -> p (n f)")[:, 0:NT]))
            dve.sem_inc(s_go, 1)

            segs = [2]

            def to_pe():
                dve.sem_inc(s_seg, 1)
                segs[0] += 1
                dve.wait_ge(s_segp, segs[0])

            def whole_segments(add, xin):
                op0, op1 = (ALU.mult, ALU.add) if add else (ALU.add, ALU.max)
                GFt, GBt = (gf, gb) if add else (gfn, gbn)
                rg, rgn, rwf, rwb = (G_, GN, WGF, WGB) if add else (GNEG, GNNEG, WGFN, WGBN)
                none = 0.0 if add else -BIG
                fl, bl = (lambda t: t.rearrange(flat2)), (lambda t: t.rearrange(flat2)[:, ::-1])
                ch.note(V.tensor_copy(seg_xf, xin))
                ch.note(V.tensor_copy(seg_xb, xin))
                ch.note(V.tensor_tensor_scan(fl(seg_f), fl(GFt[:, :, :]), fl(xin), none, op0, op1))
                ch(V.tensor_tensor_scan(bl(seg_b), bl(GBt[:, :, :]), bl(xin), none, op0, op1))
                to_pe()
                ch.note(V.tensor_tensor_scan(rscan[0], rows[:, rwf, :], row[:, 0:NT], none, op0, op1))
                ch.note(V.tensor_tensor_scan(rscan[1][:, ::-1], rows[:, rwb, ::-1], row[:, NT:2 * NT][:, ::-1], none, op0, op1))
                ch.note(V.memset(rcar[0][:, 0:1], none))
                ch.note(V.memset(rcar[1][:, NT - 1:NT], none))
                ch.join()
                ch.note(V.tensor_tensor(rcar[0][:, 1:NT], rows[:, rg, 1:NT], rscan[0][:, 0:NT - 1], op0))
                ch(V.tensor_tensor(rcar[1][:, 0:NT - 1], rows[:, rgn, 0:NT - 1], rscan[1][:, 1:NT], op0))
                to_pe()
                car = ps[4][0:Q, :, :].rearrange("p n f -> p (n f)")
                ch.note(V.tensor_tensor(seg_xf[:, :, 0], xin[:, :, 0], car[:, 400:402], op1))
                ch(V.tensor_tensor(seg_xb[:, :, R - 1], xin[:, :, R - 1], car[:, 402:404], op1))
                ch.note(V.tensor_tensor_scan(fl(seg_f), fl(GFt[:, :, :]), fl(seg_xf), none, op0, op1))
                ch(V.tensor_tensor_scan(bl(seg_b), bl(GBt[:, :, :]), bl(seg_xb), none, op0, op1))
                ch(V.tensor_tensor(seg_f, seg_f, seg_b, op1))
                if add:
                    ch(V.tensor_tensor(seg_f, seg_f, xin, ALU.subtract))

            ch(V.memset(seg_x, 1.0))
            whole_segments(True, seg_x)
            ch(V.tensor_scalar(seg_f, seg_f, 1.0, None, ALU.max))
            ch.note(V.reciprocal(lx[0][:, :, 0:R], seg_f))
            ch(V.memset(lx[0][:, :, R:P], 1.0))
            to_pe()
            ch(V.tensor_copy(invc[:, :], ps[0][:, :, :].rearrange("p n f -> p (n f)")[:, 0:NT]))
            dve.sem_inc(s_go, 1)

            for h in range(HOPS):
                c0 = h * NG
                tb = [(h + 1) * GT * 16 * (NF + (r < NG % TS)) for r in range(TS)]

                f = "p n f -> p (n f)"

                def norms(n):
                    dve.wait_ge(s_t[n.slot], 2 * GT * 16 * (n.i + 1))
                    for t in range(GT):
                        ch.note(V.bn_stats(stats[:, t, :], tr[:, n.slot * GT + t, :]))
                        ch.note(V.bn_stats(stats[:, GT + t, :], xr[:, n.slot * GT + t, :]))
                    ch.join()
                    reuse(dve, s_ohT, n.g)
                    layer_norm(P, n.u, 2 * GT, s_ln, [
                        lambda t=t: ch.note(V.tensor_scalar(oh[:, t, :], iota_c[:, :], tycol[:, n.tile(t)], None, ALU.is_equal))
                        for t in range(GT)])
                    dve.sem_inc(s_oh, 1)

                def products(n):
                    if h == 0:
                        dve.wait_ge(s_lh, n.g + 1)
                        ch.note(V.scalar_tensor_tensor(xr[:, n.ring4, :].rearrange(f), hr[:, n.ring, :].rearrange(f), 3.0,
                                                       xr[:, n.ring4, :].rearrange(f), ALU.mult, ALU.add))
                        dve.wait_ge(s_rel, n.g + 1)
                        reuse(dve, s_bs[n.u], 32 * n.nth)
                        V.tensor_copy(relr[:, n.ring, :], ps[7][:, :, :]).then_inc(s_rele, 1)
                        dve.wait_ge(s_rele, n.g + 1)
                    else:
                        dve.wait_ge(s_t[n.slot], tb[n.slot] + GT * 16 * (n.i + 1))
                        dve.wait_ge(s_rl[n.u], 16 * ((h - 1) * NI + n.nth + 1))
                        if n.back(2).exists():
                            dve.wait_ge(s_rtT, c0 + n.g - 1)
                    reuse(dve, s_cp[n.u], 16 * (h * NI + n.nth))
                    V.tensor_tensor(rtr[:, n.ring, :], tr[:, n.ring4, :], relr[:, n.ring, :], ALU.mult).then_inc(s_rt, 1)

                def scores(n):
                    dve.wait_ge(s_th, c0 + n.g + 1)
                    if h == 0:
                        dve.wait_ge(s_left, n.g + 1)
                    else:
                        dve.wait_ge(s_lf[n.u], 16 * ((h - 1) * NI + n.nth + 1))

                    def score(t):
                        k = n.u * GT + t
                        left = ps[5][:, t, :] if h == 0 else xr[:, k, :]
                        ch.note(V.scalar_tensor_tensor(thr[:, k, :], thr[:, k, :], 1.0, left, ALU.mult, ALU.mult,
                                                       accum_out=attr[:, n.u, t:t + 1]))

                    def last():
                        V.tensor_copy(att[:, n.tiles], attr[:, n.u, :]).then_inc(s_att, 1)
                    return [lambda t=t: score(t) for t in range(GT)], last

                def edges(n):
                    if h == 0:
                        if n.exists():
                            norms(n)
                        if n.back(1).exists():
                            products(n.back(1))
                    elif n.exists():
                        products(n)
                    steps, last = scores(n.back(2)) if n.back(2).exists() else ([], None)
                    if h > 0 and n.u == 1 and n.exists():
                        dense_in(h, n, steps)
                    else:
                        for one in steps:
                            one()
                        if steps:
                            ch.join()
                    if last:
                        last()
                    if h > 0 and n.u == 0 and n.back(1).exists():
                        dense_out(h, n.back(1))
                groups(dve, edges, lag=2, chain=ch)

                dve.wait_ge(s_att, c0 + NG)
                if h == 0:
                    for u in range(2):
                        dve.wait_ge(s_bs[u], 32 * NI)
                else:
                    for u in range(2):
                        dve.wait_ge(s_od[u], 16 * stored(h, u))
                to_pe()
                lin4 = ps[4][0:Q, 0:2, 0:R]
                ch(V.tensor_copy(seg_x, lin4))
                whole_segments(False, seg_x)
                V.tensor_tensor(seg_x, seg_x, seg_f, ALU.subtract).then_inc(s_exp, 1)
                dve.wait_ge(s_expd, h + 1)
                whole_segments(True, seg_x)
                ch(V.reciprocal(seg_f, seg_f))
                ch.note(V.tensor_tensor(lx[0][:, :, 0:R], seg_x, seg_f, ALU.mult))
                ch.note(V.memset(lx[0][:, :, R:R + 2], 1.0))
                ch(V.memset(lx[0][:, :, R + 2:P], 0.0))
                to_pe()
                ch(V.tensor_copy(wcol[:, :], ps[0][:, :, :].rearrange("p n f -> p (n f)")[:, 0:NT]))
                ch.note(V.tensor_tensor(wfl[:, :, 0], wcol[:, :], mfl[:, 0, :], ALU.mult))
                ch(V.tensor_tensor(wfl[:, :, 1], wcol[:, :], mfl[:, 1, :], ALU.mult))

                def partial(i, u, first=False):
                    g = vec(i, u)
                    if not first:
                        dve.wait_ge(s_bp, c0 + g - 1)
                    V.tensor_copy(wflr[:, u * GT:(u + 1) * GT, :], wfl[:, bass.ds(g * GT, GT), :]).then_inc(s_wf, 1)
                partial(0, 0, True)
                partial(0, 1, True)
                with dve.Fori(1, NI) as i:
                    partial(i, 0)
                    partial(i, 1)

                dve.wait_ge(s_part, h + 1)
                part = ps[4][:, :, :].rearrange("p n f -> p (n f)")
                ch.note(V.tensor_tensor_scan(scT[:, 0, :], bcg[:, 0, :], part[:, NT:2 * NT], 0.0, ALU.mult, ALU.add))
                ch.note(V.tensor_tensor_scan(scT[:, 1, ::-1], bcg[:, 1, ::-1], part[:, 0:NT][:, ::-1], 0.0, ALU.mult, ALU.add))
                ch.note(V.memset(cT[:, 0, 0:1], 0.0))
                ch(V.memset(cT[:, 1, NT - 1:NT], 0.0))
                ch.note(V.tensor_tensor(cT[:, 0, 1:NT], bcg[:, 2, 1:NT], scT[:, 0, 0:NT - 1], ALU.mult))
                ch(V.tensor_tensor(cT[:, 1, 0:NT - 1], bcg[:, 2, 1:NT], scT[:, 1, 1:NT], ALU.mult))
                to_pe()
                V.tensor_copy(fxr.rearrange("p b k f -> p (b k) f"), ps[5][0:Q, :, :]).then_inc(s_fix, 1)

                def weights(n):
                    m = n.back(2)
                    if m.exists():
                        dve.wait_ge(s_T, c0 + m.g + 1)
                    for t in range(GT):
                        ins = V.tensor_scalar(rtT[:, n.u * GT + t, :], segbc[:, n.tile(t), :].rearrange("p a f -> p (a f)"),
                                              lcol[:, n.tile(t)], wcol[:, n.tile(t)], ALU.is_equal, ALU.mult)
                    ins.then_inc(s_w, 1)

                def aggregate(n):
                    dve.wait_ge(s_nr, c0 + n.g + 1)
                    ch(V.tensor_scalar(nrm[:, n.u, 1, :], nrm[:, n.u, 1, :], 1e-12, None, ALU.max))
                    ch(V.reciprocal(nrm[:, n.u, 2, :], nrm[:, n.u, 1, :]))
                    ch(V.tensor_tensor(nrm[:, n.u, 3, :], nrm[:, n.u, 2, :], invc[:, n.tiles], ALU.mult))
                    if h < HOPS - 1:
                        reuse(dve, s_sc[n.slot], GT * 16 * (turn(h, n) - 1))
                    V.tensor_tensor(tr[:, n.ring4, :], ps[n.u][:, :, :], nrm[:, n.u, 3, :].unsqueeze(2).to_broadcast([P, GT, D]),
                                    ALU.mult).then_inc(s_ag, 1)

                def accumulate(n):
                    dve.wait_ge(s_al[n.slot], 16 * turn(h, n))
                    dve.wait_ge(s_ag, c0 + n.g + 1)
                    V.tensor_tensor(xr[:, n.ring4, :], xr[:, n.ring4, :], tr[:, n.ring4, :], ALU.add).then_inc(s_acc, 1)

                def sums(n):
                    m = n.back(2)
                    if m.exists():
                        aggregate(m)
                    if n.exists():
                        weights(n)
                    if m.exists():
                        accumulate(m)
                groups(dve, sums, lag=2, chain=ch)

        @block.scalar
        def _(act):
            A = nc.scalar

            def relu_rows(pr, u, src_, dst_, n0, n):
                for t in range(n):
                    ins = A.activation(dst_[0:pr, t, :], src_[0:pr, t, :], ACT.Relu, bias=lns[0:pr, u, LN_NB, n0 + t:n0 + t + 1],
                                       scale=lns[0:pr, u, LN_RS, n0 + t:n0 + t + 1])
                return ins

            for h in range(HOPS):
                c0 = h * NG

                def edges(n):
                    if h == 0 and n.exists():
                        act.wait_ge(s_ln, n.g + 1)
                        relu_rows(P, n.u, tr[:, n.ring4, :], tr[:, n.ring4, :], 0, GT)
                        relu_rows(P, n.u, xr[:, n.ring4, :], hr[:, n.ring, :], GT, GT).then_inc(s_lh, 1)
                        act.wait_ge(s_ohT, n.g + 1)
                        A.copy(ohT[:, :, :], ps[6][:, :, :]).then_inc(s_ohTs, 1)
                    m = n.back(1) if h == 0 else n
                    if m.exists():
                        if h == 0:
                            act.wait_ge(s_z, 16 * ND)
                        act.wait_ge(s_rtT, c0 + m.g + 1)
                        A.copy(rtT[:, m.ring, :], ps[m.u][:, :, :]).then_inc(s_rtTs, 1)
                        if h == 0:
                            act.wait_ge(s_hT, m.g + 1)
                            A.copy(hT[:, :, :], ps[4][:, :, :]).then_inc(s_hTs, 1)
                        act.wait_ge(s_rg, c0 + m.g + 1)
                        if m.back(2).exists():
                            act.wait_ge(s_att, c0 + m.g - 1)
                        A.activation(thr[:, m.ring, :], ps[2 + m.u][:, :, :], ACT.Tanh).then_inc(s_th, 1)
                    if h > 0 and n.u == 1 and n.exists():
                        c, w, nth = chunk(h, n)
                        act.wait_ge(s_dln, c + 1)
                        relu_rows(DR, 0, xd[w], hd, 0, DC).then_inc(s_dh, 1)
                groups(act, edges, lag=1 if h == 0 else 0)
                act.wait_ge(s_exp, h + 1)
                A.activation(seg_x, seg_x, ACT.Exp).then_inc(s_expd, 1)

                def partial_out(i):
                    for u in range(2):
                        act.wait_ge(s_bp, c0 + vec(i, u) + 1)
                        reuse(act, s_bst[u], 16 * (h * NI + i))
                        A.copy(bte[:, u, :, :], ps[u][0:2, :, :]).then_inc(s_be, 1)
                partial_out(0)
                with act.Fori(1, NI) as i:
                    partial_out(i)

                def squares(n):
                    act.wait_ge(s_T, c0 + n.g + 1)
                    for t in range(GT):
                        A.activation(rtr[:, n.u * GT + t, :], ps[n.u][:, t, :], ACT.Square, scale=invc[:, n.tile(t)],
                                     accum_out=nrm[:, n.u, 0, t:t + 1]).then_inc(s_sq, 1)
                    act.wait_ge(s_sq, GT * (c0 + n.g + 1))
                    A.activation(nrm[:, n.u, 1, :], nrm[:, n.u, 0, :], ACT.Sqrt).then_inc(s_nr, 1)

                def sums(n):
                    if n.back(1).exists():
                        squares(n.back(1))
                    if h == HOPS - 1:
                        return
                    m = n.back(2)
                    if m.exists():
                        act.wait_ge(s_aT, c0 + m.g + 1)
                        A.copy(relr[:, m.ring, :], ps[2 + m.u][:, :, :]).then_inc(s_aTs, 1)
                    m = n.back(3)
                    if m.exists():
                        act.wait_ge(s_L, c0 + m.g + 1)
                        reuse(act, s_Lst[m.u], 16 * (h * NI + m.nth))
                        A.copy(thr[:, m.ring, :], ps[4 + m.u][:, :, :]).then_inc(s_Le, 1)
                groups(act, sums, lag=3)

        @block.tensor
        def _(pe):
            T = nc.tensor
            pe.wait_ge(s_const, 3)
            with pe.Fori(0, NPH) as i:
                for way, (kk, vv) in enumerate(((kbuf[0], vbuf), (kT[0], vT))):
                    pe.wait_ge(s_srt, 2 * i + way + 1)
                    for c in range(2):
                        T.transpose(ps[0][:, c, :], kk[:, c * P:(c + 1) * P], ident[:, :])
                        ins = T.transpose(ps[1][:, c, :], vv[:, c * P:(c + 1) * P], ident[:, :])
                    ins.then_inc(s_xp, 1)

            def bank(k):
                return ps[k][:, :, :].rearrange("p n f -> p (n f)")
            pe.wait_ge(s_seg, 1)
            for k in range(2):
                for b in range(2):
                    ins = T.transpose(bank(4)[0:1, k * NT + b * Q:k * NT + (b + 1) * Q], gcol[:, k, b:b + 1], ident[0:Q, 0:Q])
            ins.then_inc(s_segp, 1)

            def to_tiles(k, out_):
                for b in range(2):
                    ins = T.transpose(out_[:, b * Q:(b + 1) * Q], lx[k][:, b, :], ident[0:Q, 0:Q])
                return ins
            pe.wait_ge(s_seg, 2)
            for k in range(7):
                to_tiles(k, bank(k // 2)[:, (k % 2) * NT:(k % 2 + 1) * NT])
            T.matmul(bank(5)[:, 0:2 * NT], onesr[:, :], rows[:, WGF:WGB + 1, :].rearrange("p k n -> p (k n)"), start=True, stop=True)
            T.matmul(bank(6)[:, 0:NT], onesr[:, :], rows[:, G_, :], start=True, stop=True).then_inc(s_segp, 1)

            segs = [2]

            def asked():
                segs[0] += 1
                pe.wait_ge(s_seg, segs[0])

            def whole_segments():
                asked()
                for k, (t, r) in enumerate(((seg_f, R - 1), (seg_b, 0))):
                    for b in range(2):
                        ins = T.transpose(bank(4)[0:1, k * NT + b * Q:k * NT + (b + 1) * Q], t[:, b, r:r + 1], ident[0:Q, 0:Q])
                ins.then_inc(s_segp, 1)
                asked()
                for k in range(2):
                    for b in range(2):
                        ins = T.transpose(bank(4)[0:Q, 400 + 2 * k + b:401 + 2 * k + b], rcar[k][:, b * Q:(b + 1) * Q], ident[0:1, 0:1])
                ins.then_inc(s_segp, 1)

            def weights_to_tiles():
                asked()
                to_tiles(0, bank(0)[:, 0:NT]).then_inc(s_segp, 1)
            whole_segments()
            weights_to_tiles()

            for h in range(HOPS):
                c0 = h * NG
                def edges(n):
                    if h == 0 and n.exists():
                        pe.wait_ge(s_oh, n.g + 1)
                        for t in range(GT):
                            ins = T.transpose(ps[6][:, t, :], oh[:, t, :], ident[:, :])
                        ins.then_inc(s_ohT, 1)
                        pe.wait_ge(s_ohTs, n.g + 1)
                        reuse(pe, s_rele, n.g)
                        for t in range(GT):
                            ins = T.matmul(ps[7][:, t, :], ohT[:, t, :], emb[:, :], start=True, stop=True)
                        ins.then_inc(s_rel, 1)
                    m = n.back(1) if h == 0 else n
                    if not m.exists():
                        return
                    pe.wait_ge(s_rt, c0 + m.g + 1)
                    for t in range(GT):
                        ins = T.transpose(ps[m.u][:, t, :], rtr[:, m.u * GT + t, :], ident[:, :])
                    ins.then_inc(s_rtT, 1)
                    if h == 0:
                        pe.wait_ge(s_lh, m.g + 1)
                        for t in range(GT):
                            ins = T.transpose(ps[4][:, t, :], hr[:, m.u * GT + t, :], ident[:, :])
                        ins.then_inc(s_hT, 1)
                    pe.wait_ge(s_rtTs, c0 + m.g + 1)
                    if m.back(2).exists():
                        pe.wait_ge(s_th, c0 + m.g - 1)
                    for t in range(GT):
                        ins = T.matmul(ps[2 + m.u][:, t, :], rtT[:, m.u * GT + t, :], kw[:, :], start=True, stop=True)
                    ins.then_inc(s_rg, 1)
                    if h == 0:
                        pe.wait_ge(s_hTs, m.g + 1)
                        reuse(pe, s_att, m.g)
                        for t in range(GT):
                            ins = T.matmul(ps[5][:, t, :], hT[:, t, :], qw[:, :], start=True, stop=True)
                        ins.then_inc(s_left, 1)
                groups(pe, edges, lag=1 if h == 0 else 0)

                asked()
                for b in range(2):
                    ins = T.transpose(ps[4][0:Q, b, :], att[:, b * Q:(b + 1) * Q], ident[:, :])
                ins.then_inc(s_segp, 1)
                whole_segments()
                whole_segments()
                weights_to_tiles()

                for u in range(2):
                    pe.wait_ge(s_cp[u], 16 * NI * (h + 1))

                def partial(i, u, first=False):
                    g = vec(i, u)
                    pe.wait_ge(s_wf, c0 + g + 1)
                    if not first:
                        pe.wait_ge(s_be, c0 + g - 1)
                    for t in range(GT):
                        ins = T.matmul(ps[u][0:2, t, :], wflr[:, u * GT + t, :],
                                       rt[:, bass.ds(g * GT + t, 1), :].rearrange("p a f -> p (a f)"), start=True, stop=True)
                    ins.then_inc(s_bp, 1)
                partial(0, 0, True)
                partial(0, 1, True)
                with pe.Fori(1, NI) as i:
                    partial(i, 0)
                    partial(i, 1)
                pe.wait_ge(s_rd, 48 + 48 * h + 32)
                for k in range(2):
                    for b in range(2):
                        ins = T.transpose(bank(4)[:, k * NT + b * Q:k * NT + (b + 1) * Q], btr[:, b, k, :], ident[0:Q, 0:Q])
                ins.then_inc(s_part, 1)
                asked()
                for k in range(2):
                    for b in range(2):
                        ins = T.transpose(ps[5][0:Q, 2 * b + k, :], cT[:, k, b * Q:(b + 1) * Q], ident[:, :])
                ins.then_inc(s_segp, 1)
                pe.wait_ge(s_rd, 48 + 48 * (h + 1))

                def sums(n):
                    m = n.back(1)
                    if m.exists():
                        pe.wait_ge(s_w, c0 + m.g + 1)
                        if m.back(2).exists():
                            pe.wait_ge(s_ag, c0 + m.g - 1)
                        for t in range(GT):
                            ins = T.matmul(ps[m.u][:, t, :], rtT[:, m.u * GT + t, :],
                                           rt[:, m.tile(t), :].rearrange("p a f -> p (a f)"), start=True, stop=True)
                        ins.then_inc(s_T, 1)
                    if h == HOPS - 1:
                        return
                    m = n.back(3)
                    if m.exists():
                        pe.wait_ge(s_aTs, c0 + m.g + 1)
                        if m.back(2).exists():
                            pe.wait_ge(s_Le, c0 + m.g - 1)
                        for t in range(GT):
                            ins = T.matmul(ps[4 + m.u][:, t, :], relr[:, m.u * GT + t, :], qw[:, :], start=True, stop=True)
                        ins.then_inc(s_L, 1)
                    m = n.back(2)
                    if m.exists():
                        pe.wait_ge(s_ag, c0 + m.g + 1)
                        for t in range(GT):
                            ins = T.transpose(ps[2 + m.u][:, t, :], tr[:, m.slot * GT + t, :], ident[:, :])
                        ins.then_inc(s_aT, 1)
                groups(pe, sums, lag=3)


_INS = ['x', 'src', 'dst', 'edge_type_64', 'L0_gnn_edge_emb', 'L0_gnn_q_w', 'L0_gnn_k_w']


def kernel(**inputs):
    import numpy as _np
    import concourse.bacc as _bacc
    from concourse import mybir as _mybir
    from concourse.bass_utils import run_bass_kernel_spmd as _run

    nc = _bacc.Bacc("TRN2", target_bir_lowering=False, num_devices=1)
    arrays, args = {}, []
    for name in _INS:
        a = _np.ascontiguousarray(inputs[name])
        arrays[f"in_{name}_dram"] = a
        args.append(nc.dram_tensor(f"in_{name}_dram", a.shape, _mybir.dt.from_np(a.dtype), kind="ExternalInput").ap())
    args.append(nc.dram_tensor("out_0_dram", (50000, 128), _mybir.dt.float32, kind="ExternalOutput").ap())
    gnn_kernel(nc, *args)
    r = _run(nc, [arrays], core_ids=[0])
    return r.results[0]["out_0_dram"]
```
